# Optimizing a Trainium2 kernel written in Bass

```python
import numpy as np
import jax
import jax.numpy as jnp

def _softmax(x, axis=-1):
    return jax.nn.softmax(x, axis=axis)

def _gelu(x):
    return jax.nn.gelu(x, approximate=True)

def _silu(x):
    return jax.nn.silu(x)

def _sigmoid(x):
    return jax.nn.sigmoid(x)

def _layernorm(x, axis=-1, eps=1e-05):
    m = jnp.mean(x, axis=axis, keepdims=True)
    v = jnp.var(x, axis=axis, keepdims=True)
    return (x - m) / jnp.sqrt(v + eps)

def _scatter_add(tgt, idx, src, axis=0):
    return tgt.at[idx].add(src)

def _segment_sum(src, seg, n):
    return jax.ops.segment_sum(src, seg, n)
kernel_name = 'mk_xattn_ffn_d1_seqx_r8_83caf0'

def setup_inputs(seed: int=0):
    np.random.seed(seed)
    _w = jnp.asarray

    def _rec_inputs():
        import jax
        import jax.numpy as jnp
        _rk = jax.random.key(seed)
        x = -0.0003929 + 0.9999 * jax.random.normal(jax.random.fold_in(_rk, 1), (32, 64, 512), jnp.float32)
        _lenS = 64 - jax.random.randint(jax.random.fold_in(_rk, 7), (32,), 0, max(1, 64 // 4) + 1, jnp.int32)
        _lenS2 = 64 - jax.random.randint(jax.random.fold_in(_rk, 8), (32,), 0, max(1, 64 // 4) + 1, jnp.int32)
        _ctx_4096P = jax.random.normal(jax.random.fold_in(_rk, 11), (32, 16, 512), jnp.float32)
        _ctx_4096c = jax.random.dirichlet(jax.random.fold_in(_rk, 511), 0.3 * jnp.ones((16,), jnp.float32), (32, 64))
        _ctx_4096t = jnp.einsum('bsk,bkd->bsd', _ctx_4096c, _ctx_4096P)
        _ctx_4096t = _ctx_4096t * jax.lax.rsqrt(jnp.mean(jnp.square(_ctx_4096t)) + 1e-12) * 0.953939
        ctx_4096 = 2.81802e-05 + 1.00001 * (_ctx_4096t + 0.3 * jax.random.normal(jax.random.fold_in(_rk, 611), (32, 64, 512), jnp.float32))
        return (x, ctx_4096)
    x, ctx_4096 = _rec_inputs()

    def _L0_xattn_setup():
        import jax, jax.numpy as jnp
        import numpy as np
        DIM = 64
        HEADS = 8
        DIM_HEAD = 64
        HIDDEN = HEADS * DIM_HEAD
        SCALE = DIM_HEAD ** (-0.5)
        key = jax.random.key(seed)
        ks = jax.random.split(key, 9)
        b, n = (8, 512)
        std = 1.0 / np.sqrt(DIM)
        return {'q': jax.random.normal(ks[0], (b, DIM, n), jnp.float32), 'k': jax.random.normal(ks[1], (b, DIM, n), jnp.float32), 'v': jax.random.normal(ks[2], (b, DIM, n), jnp.float32), 'Wq': jax.random.normal(ks[3], (HIDDEN, DIM), jnp.float32) * std, 'Wk': jax.random.normal(ks[4], (HIDDEN, DIM), jnp.float32) * std, 'Wv': jax.random.normal(ks[5], (HIDDEN, DIM), jnp.float32) * std, 'Wo': jax.random.normal(ks[6], (DIM, HIDDEN), jnp.float32) * (1.0 / np.sqrt(HIDDEN)), 'bo': jax.random.normal(ks[7], (DIM,), jnp.float32) * 0.01, 'g': jnp.ones((1, DIM, 1), jnp.float32)}
    _L0_xattn_all = _L0_xattn_setup()
    _L0_xattn_in = {k: v for k, v in _L0_xattn_all.items() if k in ('Wq', 'Wk', 'Wv', 'Wo', 'bo', 'g')}
    del _L0_xattn_all

    def _L0_ffn_setup():
        import jax, jax.numpy as jnp
        import numpy as np
        IN, OUT = (512, 512)
        R_TOP, R_INT = (64, 4)
        R_TAIL = min(IN, OUT) - R_TOP
        B, S = (4, 128)
        key = jax.random.key(seed)
        ks = jax.random.split(key, 10)
        sc = 1.0 / np.sqrt(OUT)
        x = jax.random.normal(ks[0], (B, S, IN), jnp.float32)
        U_top = jax.random.normal(ks[1], (OUT, R_TOP), jnp.float32) * sc
        Vh_top = jax.random.normal(ks[2], (R_TOP, IN), jnp.float32) * sc
        U_tail = jax.random.normal(ks[3], (OUT, R_TAIL), jnp.float32) * sc
        Vh_tail = jax.random.normal(ks[4], (R_TAIL, IN), jnp.float32) * sc
        S_top = jnp.sort(jax.random.uniform(ks[5], (R_TOP,), jnp.float32, 1.0, 10.0))[::-1]
        S_tail = jnp.sort(jax.random.uniform(ks[6], (R_TAIL,), jnp.float32, 0.01, 1.0))[::-1]
        U_tail_r = U_tail[:, :R_INT]
        S_tail_r = S_tail[:R_INT]
        Vh_tail_r = Vh_tail[:R_INT, :]
        alpha = jnp.ones((R_TOP,), jnp.float32)
        beta = jnp.zeros((R_TOP,), jnp.float32)
        D = jnp.ones((R_INT,), jnp.float32)
        R = jnp.eye(R_INT, dtype=jnp.float32) + 0.01 * jax.random.normal(ks[7], (R_INT, R_INT), jnp.float32)
        bias = jax.random.normal(ks[8], (OUT,), jnp.float32) * 0.02
        return dict(x=x, U_top=U_top, S_top=S_top, Vh_top=Vh_top, U_tail=U_tail, S_tail=S_tail, Vh_tail=Vh_tail, U_tail_r=U_tail_r, S_tail_r=S_tail_r, Vh_tail_r=Vh_tail_r, alpha=alpha, beta=beta, D=D, R=R, bias=bias)
    _L0_ffn_all = _L0_ffn_setup()
    _L0_ffn_in = {k: v for k, v in _L0_ffn_all.items() if k in ('U_top', 'S_top', 'Vh_top', 'U_tail', 'S_tail', 'Vh_tail', 'U_tail_r', 'S_tail_r', 'Vh_tail_r', 'alpha', 'beta', 'D', 'R', 'bias')}
    del _L0_ffn_all
    return {'x': x, 'ctx_4096': ctx_4096, 'L0_xattn_Wq': _L0_xattn_in['Wq'], 'L0_xattn_Wk': _L0_xattn_in['Wk'], 'L0_xattn_Wv': _L0_xattn_in['Wv'], 'L0_xattn_Wo': _L0_xattn_in['Wo'], 'L0_xattn_bo': _L0_xattn_in['bo'], 'L0_xattn_g': _L0_xattn_in['g'], 'L0_ffn_U_top': _L0_ffn_in['U_top'], 'L0_ffn_S_top': _L0_ffn_in['S_top'], 'L0_ffn_Vh_top': _L0_ffn_in['Vh_top'], 'L0_ffn_U_tail': _L0_ffn_in['U_tail'], 'L0_ffn_S_tail': _L0_ffn_in['S_tail'], 'L0_ffn_Vh_tail': _L0_ffn_in['Vh_tail'], 'L0_ffn_U_tail_r': _L0_ffn_in['U_tail_r'], 'L0_ffn_S_tail_r': _L0_ffn_in['S_tail_r'], 'L0_ffn_Vh_tail_r': _L0_ffn_in['Vh_tail_r'], 'L0_ffn_alpha': _L0_ffn_in['alpha'], 'L0_ffn_beta': _L0_ffn_in['beta'], 'L0_ffn_D': _L0_ffn_in['D'], 'L0_ffn_R': _L0_ffn_in['R'], 'L0_ffn_bias': _L0_ffn_in['bias']}

def reference(x, ctx_4096, L0_xattn_Wq, L0_xattn_Wk, L0_xattn_Wv, L0_xattn_Wo, L0_xattn_bo, L0_xattn_g, L0_ffn_U_top, L0_ffn_S_top, L0_ffn_Vh_top, L0_ffn_U_tail, L0_ffn_S_tail, L0_ffn_Vh_tail, L0_ffn_U_tail_r, L0_ffn_S_tail_r, L0_ffn_Vh_tail_r, L0_ffn_alpha, L0_ffn_beta, L0_ffn_D, L0_ffn_R, L0_ffn_bias):
    import jax
    import jax.numpy as jnp

    def _L0_xattn_ref(q, k, v, Wq, Wk, Wv, Wo, bo, g):
        import jax, jax.numpy as jnp
        import numpy as np
        DIM = 64
        HEADS = 8
        DIM_HEAD = 64
        HIDDEN = HEADS * DIM_HEAD
        SCALE = DIM_HEAD ** (-0.5)
        b = q.shape[0]
        qh = jnp.einsum('bcn,oc->bon', q, Wq).reshape(b, HEADS, DIM_HEAD, -1)
        kh = jnp.einsum('bcn,oc->bon', k, Wk).reshape(b, HEADS, DIM_HEAD, -1)
        vh = jnp.einsum('bcn,oc->bon', v, Wv).reshape(b, HEADS, DIM_HEAD, -1)
        qh = jax.nn.softmax(qh, axis=-2) * SCALE
        kh = jax.nn.softmax(kh, axis=-1)
        context = jnp.einsum('bhdn,bhen->bhde', kh, vh)
        out = jnp.einsum('bhde,bhdn->bhen', context, qh)
        out = out.reshape(b, HIDDEN, -1)
        out = jnp.einsum('bcn,oc->bon', out, Wo) + bo[None, :, None]
        norm = jnp.maximum(jnp.sqrt(jnp.sum(out * out, axis=1, keepdims=True)), 1e-12)
        return out / norm * g * np.sqrt(DIM)

    def _L0_ffn_ref(x, U_top, S_top, Vh_top, U_tail, S_tail, Vh_tail, U_tail_r, S_tail_r, Vh_tail_r, alpha, beta, D, R, bias):
        import jax, jax.numpy as jnp
        import numpy as np
        IN, OUT = (512, 512)
        R_TOP, R_INT = (64, 4)
        R_TAIL = min(IN, OUT) - R_TOP
        B, S = (4, 128)
        s_head = jax.nn.relu(S_top * alpha + beta)
        W_head = U_top * s_head[None, :] @ Vh_top
        W_tail = U_tail * S_tail[None, :] @ Vh_tail
        Bm = U_tail_r * S_tail_r[None, :]
        delta = Bm * jax.nn.relu(D)[None, :] @ R @ Vh_tail_r
        W_eff = W_head + W_tail + delta
        return jnp.einsum('bsi,oi->bso', x, W_eff) + bias
    x = x + _L0_xattn_ref(_layernorm(x, axis=-1), ctx_4096, ctx_4096, L0_xattn_Wq, L0_xattn_Wk, L0_xattn_Wv, L0_xattn_Wo, L0_xattn_bo, L0_xattn_g)
    x = x + _L0_ffn_ref(_layernorm(x, axis=-1), L0_ffn_U_top, L0_ffn_S_top, L0_ffn_Vh_top, L0_ffn_U_tail, L0_ffn_S_tail, L0_ffn_Vh_tail, L0_ffn_U_tail_r, L0_ffn_S_tail_r, L0_ffn_Vh_tail_r, L0_ffn_alpha, L0_ffn_beta, L0_ffn_D, L0_ffn_R, L0_ffn_bias)
    return x

_drawn_inputs = setup_inputs


def setup_inputs(seed=0):
    import zlib

    import numpy as np

    out = dict(_drawn_inputs(seed))
    spreads = {'L0_xattn_g': (1.0, 0.2),
     'L0_ffn_alpha': (1.0, 0.2),
     'L0_ffn_beta': (0.0, 0.625),
     'L0_ffn_D': (1.0, 0.6)}
    factors = {'L0_ffn_S_tail_r': 8.0, 'L0_ffn_R': 2.728, 'L0_ffn_bias': 8.0}
    for name, (base, spread) in spreads.items():
        noise = np.random.default_rng([zlib.crc32(name.encode()), seed]).standard_normal(out[name].shape)
        drawn = base * np.exp(spread * noise) if base else spread * noise
        out[name] = jnp.asarray(drawn.astype(out[name].dtype))
    for name, factor in factors.items():
        out[name] = (out[name] * factor).astype(out[name].dtype)
    return out
```

```python
from contextlib import ExitStack

import concourse.bass as bass
from concourse import mybir

ALU = mybir.AluOpType
ACT = mybir.ActivationFunctionType
AX = mybir.AxisListType
F32 = mybir.dt.float32
F32R = mybir.dt.float32r

P = 128
BATCH, C, N = 32, 64, 512
HEADS, DH = 8, 64
HID = HEADS * DH
PAIRS = BATCH // 2
TILES = HID // P
CHUNKS = N // P
U = 2 * TILES
R_TOP, R_INT = 64, 4
R_TAIL = N - R_TOP
SCALE = float(DH) ** -0.5
LN_EPS = 1e-5
NORM_EPS = 1e-12
BANK = 512


def xattn_ffn(nc, x, ctx, Wq, Wk, Wv, Wo, bo, g, U_top, S_top, Vh_top, U_tail, S_tail, Vh_tail,
              U_tail_r, S_tail_r, Vh_tail_r, alpha, beta, D, R, bias, out):
    es = ExitStack()
    with es:
        def sb(name, shape, dt=F32):
            return es.enter_context(nc.sbuf_tensor(name, shape, dt))

        def sem(name):
            return es.enter_context(nc.semaphore(name))

        def bank(name):
            return es.enter_context(nc.psum_tensor(name, [P, BANK], F32))

        ps_kl = bank("ps_kl")
        ps_ql = bank("ps_ql")
        ps_kt = bank("ps_kt")
        ps_qt = bank("ps_qt")
        ps_m = bank("ps_m")
        ps_o = bank("ps_o")
        ps_x0 = bank("ps_x0")
        ps_x1 = bank("ps_x1")
        banks = [ps_kl, ps_ql, ps_kt, ps_qt, ps_m, ps_o, ps_x0, ps_x1]

        ident = sb("ident", [P, P])
        ident_r = sb("ident_r", [P, P], F32R)
        batch_of = sb("batch_of", [P, 2])
        minus_half = sb("minus_half", [P, 2 * CHUNKS])
        U_sb = sb("U_sb", [P, 4, N])
        Ur_sb = sb("Ur_sb", [P, 4, R_INT])
        UT = sb("UT", [P, 4, N])
        Vh_sb = sb("Vh_sb", [P, 4, N])
        Vhr_sb = sb("Vhr_sb", [R_INT, N])
        R_sb = sb("R_sb", [R_INT, R_INT])
        s_col = sb("s_col", [P, 4])
        head_col = sb("head_col", [R_TOP, 4])
        tail_col = sb("tail_col", [R_INT, 3])
        BmT = sb("BmT", [R_INT, N])
        RBmT = sb("RBmT", [R_INT, N])
        Wff_hi = sb("Wff_hi", [P, 4, N], F32R)
        Wff_lo = sb("Wff_lo", [P, 4, N], F32R)
        Wq_dup = sb("Wq_dup", [P, TILES, 2 * C])
        Wk_dup = sb("Wk_dup", [P, TILES, 2 * C])
        WqT_hi = sb("WqT_hi", [P, HID], F32R)
        WqT_lo = sb("WqT_lo", [P, HID], F32R)
        WkT_hi = sb("WkT_hi", [P, HID], F32R)
        WkT_lo = sb("WkT_lo", [P, HID], F32R)
        Wv_sb = sb("Wv_sb", [P, TILES, C])
        Wo_sb = sb("Wo_sb", [C, HID])
        WoT = sb("WoT", [P, TILES, C])
        VO = sb("VO", [P, HEADS, C])
        g_col = sb("g_col", [P, 1])
        g8 = sb("g8", [P, 1])
        bo_col = sb("bo_col", [P, 1])
        bias_bc = sb("bias_bc", [P, N])

        xin = sb("xin", [P, N])
        cin = sb("cin", [P, N])
        xres = sb("xres", [P, N])
        xhat = sb("xhat", [P, N])
        x_hi = sb("x_hi", [P, N], F32R)
        x_lo = sb("x_lo", [P, N], F32R)
        c_hi = sb("c_hi", [P, N], F32R)
        c_lo = sb("c_lo", [P, N], F32R)
        xs = [sb(f"xs{i}", [P, 2, N], F32R) for i in range(2)]
        cs = [sb(f"cs{i}", [P, 2, N], F32R) for i in range(2)]
        ctxT = sb("ctxT", [P, CHUNKS, P])
        st1 = sb("st1", [P, 6])
        mv1 = sb("mv1", [P, 2])
        var1 = sb("var1", [P, 1])
        rstd1 = sb("rstd1", [P, 1])
        nm_k = sb("nm_k", [P, U])
        sum_k = [sb(f"sum_k{i}", [P, 2, TILES]) for i in range(2)]
        rk = sb("rk", [P, 2, TILES])
        ek = [sb(f"ek{i}", [P, N]) for i in range(2)]
        ekT = [sb(f"ekT{i}", [P, CHUNKS, P]) for i in range(4)]
        nm_q = [sb(f"nm_q{i}", [P, HEADS], F32R) for i in range(2)]
        eq = [sb(f"eq{i}", [P, HEADS, DH]) for i in range(2)]
        sum_q = [sb(f"sum_q{i}", [P, HEADS]) for i in range(2)]
        rq = [sb(f"rq{i}", [P, HEADS]) for i in range(2)]
        qn = [sb(f"qn{i}", [P, HEADS, DH]) for i in range(2)]
        qT = [sb(f"qT{i}", [P, TILES, P]) for i in range(8)]
        M_sb = sb("M_sb", [P, HID])
        G_sb = sb("G_sb", [P, 2, TILES, C])
        o_sb = sb("o_sb", [P, N])
        o_sq = sb("o_sq", [P, N])
        ssq_c = sb("ssq_c", [P, CHUNKS, 2])
        rnorm = sb("rnorm", [P, CHUNKS, 2])
        on = sb("on", [P, N])
        x1 = sb("x1", [P, N])
        x1b = sb("x1b", [P, N])
        st2 = sb("st2", [P, 6])
        mv2 = sb("mv2", [P, 2])
        var2 = sb("var2", [P, 1])
        rstd2 = sb("rstd2", [P, 1])
        x1hat = sb("x1hat", [P, N])
        zT_hi = sb("zT_hi", [P, 4, P], F32R)
        zT_lo = sb("zT_lo", [P, 4, P], F32R)
        y = sb("y", [P, N])

        w_in = sem("w_in")
        const_a = sem("const_a")
        prep_col = sem("prep_col")
        prep_mm = sem("prep_mm")
        prep_sb = sem("prep_sb")
        prep_hi = sem("prep_hi")
        xin_in, cin_in, xres_in = sem("xin_in"), sem("cin_in"), sem("xres_in")
        x_mv, x_var, x_rs, x_hat = sem("x_mv"), sem("x_var"), sem("x_rs"), sem("x_hat")
        x_hi_ok, x_lo_ok, c_hi_ok, c_lo_ok = sem("x_hi_ok"), sem("x_lo_ok"), sem("c_hi_ok"), sem("c_lo_ok")
        xs_in, cs_in = sem("xs_in"), sem("cs_in")
        k_logits, k_max, k_exp = sem("k_logits"), sem("k_max"), sem("k_exp")
        k_tr, k_trsb = sem("k_tr"), sem("k_trsb")
        ctx_tr, ctx_trsb = sem("ctx_tr"), sem("ctx_trsb")
        m_done, m_sb, rk_ok = sem("m_done"), sem("m_sb"), sem("rk_ok")
        g_done, g_sb = sem("g_done"), sem("g_sb")
        q_logits, q_max, q_shift, q_exp = sem("q_logits"), sem("q_max"), sem("q_shift"), sem("q_exp")
        q_sum, q_rec, q_norm, q_tr, q_trsb = sem("q_sum"), sem("q_rec"), sem("q_norm"), sem("q_tr"), sem("q_trsb")
        o_done, o_ok, sq_ok, ssq_done = sem("o_done"), sem("o_ok"), sem("sq_ok"), sem("ssq_done")
        ssq_ok, rn_ok, rn_bc = sem("ssq_ok"), sem("rn_ok"), sem("rn_bc")
        on_ok, x1_ok, x1b_ok = sem("on_ok"), sem("x1_ok"), sem("x1b_ok")
        z_mv, z_var, z_rs, z_ok = sem("z_mv"), sem("z_var"), sem("z_rs"), sem("z_ok")
        z_tr, z_hi, z_lo = sem("z_tr"), sem("z_hi"), sem("z_lo")
        ffn_done, y_ok, y_out = sem("ffn_done"), sem("y_ok"), sem("y_out")

        x_d = x.rearrange("(q b) c n -> q (b c) n", b=2)
        ctx_d = ctx.rearrange("(q b) c n -> q (b c) n", b=2)
        out_d = out.rearrange("(q b) c n -> q (b c) n", b=2)

        def wait(eng, s, value):
            if isinstance(value, int) and value <= 0:
                return
            eng.wait_ge(s, value)

        def steps(eng, step):
            step(-1, 1, True, False, False, False)
            step(0, 0, True, True, False, False)
            step(1, 1, True, True, True, False)
            with eng.Fori(1, PAIRS // 2 - 1) as i:
                step(2 * i, 0, True, True, True, True)
                step(2 * i + 1, 1, True, True, True, True)
            step(PAIRS - 2, 0, True, True, True, True)
            step(PAIRS - 1, 1, False, True, True, True)
            step(PAIRS, 0, False, False, True, True)
            step(PAIRS + 1, 1, False, False, False, True)

        block = es.enter_context(nc.Block())

        W_LOADS = 0

        @block.sync
        def _(sp):
            nonlocal W_LOADS

            def load(dst, src):
                nonlocal W_LOADS
                sp.dma_start(dst, src).then_inc(w_in, 16)
                W_LOADS += 1

            def load_pair(dst, src, s):
                sp.dma_start(dst, src).then_inc(s, 16)

            def col(v):
                return v.rearrange("(n a) -> n a", a=1)

            sp.dma_start(cin[:], ctx_d[0]).then_inc(cin_in, 16)
            sp.dma_start(xin[:], x_d[0]).then_inc(xin_in, 16)
            for w, src in ((Wk_dup, Wk), (Wq_dup, Wq)):
                for d in range(2):
                    load(w[:, :, d * C:(d + 1) * C], src.rearrange("(t p) c -> p t c", p=P))
            load(Wv_sb[:], Wv.rearrange("(t p) c -> p t c", p=P))
            load(Wo_sb[:], Wo)
            for b in range(2):
                load(bo_col[b * C:(b + 1) * C, :], col(bo))
                load(g_col[b * C:(b + 1) * C, :], g[0])
            load(U_sb[:, :, 0:R_TOP], U_top.rearrange("(t p) r -> p t r", p=P))
            load(U_sb[:, :, R_TOP:N], U_tail.rearrange("(t p) r -> p t r", p=P))
            load(Ur_sb[:], U_tail_r.rearrange("(t p) r -> p t r", p=P))
            load(Vh_sb[0:R_TOP, 0, :], Vh_top)
            load(Vh_sb[R_TOP:P, 0, :], Vh_tail[0:P - R_TOP, :])
            load(Vh_sb[:, 1:4, :], Vh_tail[P - R_TOP:R_TAIL, :].rearrange("(t p) i -> p t i", p=P))
            load(Vhr_sb[:], Vh_tail_r)
            load(R_sb[:], R)
            load(head_col[:, 0:1], col(S_top))
            load(head_col[:, 1:2], col(alpha))
            load(head_col[:, 2:3], col(beta))
            load(tail_col[:, 0:1], col(S_tail_r))
            load(tail_col[:, 1:2], col(D))
            load(s_col[R_TOP:P, 0:1], col(S_tail[0:P - R_TOP]))
            for t in range(1, 4):
                a = P - R_TOP + (t - 1) * P
                load(s_col[:, t:t + 1], col(S_tail[a:a + P]))
            load(bias_bc[:], bias.rearrange("(a n) -> a n", a=1).to_broadcast([P, N]))

            def load_cin(q):
                wait(sp, c_lo_ok, q)
                wait(sp, c_hi_ok, q)
                wait(sp, ctx_tr, q)
                sp.dma_start(cin[:], ctx_d[q]).then_inc(cin_in, 16)

            def load_xin(q):
                wait(sp, x_hat, q)
                sp.dma_start(xin[:], x_d[q]).then_inc(xin_in, 16)

            def stack(q, par, hi, lo, hi_ok, lo_ok, dst, landed):
                wait(sp, hi_ok, q + 1)
                wait(sp, lo_ok, q + 1)
                for b in range(2):
                    sp.dma_start(dst[par][0:C, b, :].bitcast(F32), hi[b * C:(b + 1) * C, :].bitcast(F32)).then_inc(landed, 16)
                    sp.dma_start(dst[par][C:P, b, :].bitcast(F32), lo[b * C:(b + 1) * C, :].bitcast(F32)).then_inc(landed, 16)

            stack(0, 0, c_hi, c_lo, c_hi_ok, c_lo_ok, cs, cs_in)

            def step(p, par, do_k, do_q, do_fin, do_ffn):
                if do_k:
                    if not (isinstance(p, int) and p == -1):
                        load_xin(p + 1)
                    stack(p + 1, 1 - par, x_hi, x_lo, x_hi_ok, x_lo_ok, xs, xs_in)
                    if not (isinstance(p, int) and p + 2 >= PAIRS):
                        load_cin(p + 2)
                        stack(p + 2, par, c_hi, c_lo, c_hi_ok, c_lo_ok, cs, cs_in)
                if do_fin:
                    wait(sp, x1_ok, p - 1)
                    sp.dma_start(xres[:], x_d[p - 1]).then_inc(xres_in, 16)
                if do_ffn:
                    wait(sp, y_ok, p - 1)
                    sp.dma_start(out_d[p - 2], y[:]).then_inc(y_out, 16)

            steps(sp, step)
            sp.wait_ge(y_out, 16 * PAIRS)

        @block.gpsimd
        def _(pool):
            pool.memset(ident[:], 0.0).then_inc(const_a, 1)
            pool.memset(batch_of[:], 0.0).then_inc(const_a, 1)
            pool.memset(minus_half[:], -0.5).then_inc(const_a, 1)
            pool.wait_ge(const_a, 3)
            pool.affine_select(out=ident[:], in_=ident[:], compare_op=ALU.not_equal, fill=1.0, base=0,
                               pattern=[[-1, P]], channel_multiplier=1).then_inc(const_a, 1)
            for b in range(2):
                pool.wait_ge(const_a, 4 + b)
                pool.memset(batch_of[b * C:(b + 1) * C, b:b + 1], 1.0).then_inc(const_a, 1)
            pool.wait_ge(const_a, 6)

            def c_low(q):
                pool.wait_ge(c_hi_ok, q + 1)
                wait(pool, cs_in, 64 * q)
                pool.tensor_tensor(c_lo[:], cin[:], c_hi[:], ALU.subtract).then_inc(c_lo_ok, 1)

            def x_low(q):
                pool.wait_ge(x_hi_ok, q + 1)
                wait(pool, xs_in, 64 * q)
                pool.tensor_tensor(x_lo[:], xhat[:], x_hi[:], ALU.subtract).then_inc(x_lo_ok, 1)

            c_low(0)

            def x_rstd(q):
                pool.wait_ge(x_var, q + 1)
                pool.tensor_tensor(rstd1[:], var1[:], minus_half[:, 0:1], ALU.pow).then_inc(x_rs, 1)

            def norm(q, u):
                v = U * q + u
                pool.wait_ge(q_rec, v + 1)
                wait(pool, q_tr, v - 1)
                pool.tensor_tensor(qn[u % 2][:], eq[u % 2][:], rq[u % 2][:].unsqueeze(2).to_broadcast([P, HEADS, DH]),
                                   ALU.mult).then_inc(q_norm, 1)

            def step(p, par, do_k, do_q, do_fin, do_ffn):
                for u in range(U):
                    if do_q and u > 0:
                        norm(p, u - 1)
                    if u == 0 and not (isinstance(p, int) and p <= 0) and (do_q or not do_k and do_fin):
                        norm(p - 1, U - 1)
                    if u == 1 and do_k:
                        x_rstd(p + 1)
                    if u == 3 and do_k:
                        x_low(p + 1)
                    if u == 4 and do_fin:
                        pool.wait_ge(o_ok, p)
                        pool.tensor_tensor(o_sq[:], o_sb[:], o_sb[:], ALU.mult).then_inc(sq_ok, 1)
                    if u == 5 and do_fin:
                        pool.wait_ge(ssq_ok, p)
                        pool.tensor_tensor(rnorm[:], ssq_c[:], minus_half[:].rearrange("p (j b) -> p j b", b=2),
                                           ALU.pow).then_inc(rn_ok, 1)
                    if u == 6 and do_k and not (isinstance(p, int) and p + 2 >= PAIRS):
                        c_low(p + 2)
                    if u == 6 and do_fin:
                        pool.wait_ge(z_var, p)
                        pool.tensor_tensor(rstd2[:], var2[:], minus_half[:, 0:1], ALU.pow).then_inc(z_rs, 1)
                    if u == 7 and do_fin:
                        pool.wait_ge(x1_ok, p)
                        wait(pool, y_ok, p - 1)
                        pool.tensor_tensor(x1b[:], x1[:], bias_bc[:], ALU.add).then_inc(x1b_ok, 1)

            pool.wait_ge(w_in, 16 * W_LOADS)
            steps(pool, step)

        @block.tensor
        def _(pe):
            n_prep = [0]

            def prep(run, needs=0):
                n = n_prep[0]
                n_prep[0] += 1
                wait(pe, prep_sb, max(needs, n - len(banks) + 1))
                run(banks[n % len(banks)]).then_inc(prep_mm, 1)

            def transposes(tiles):
                def run(ps):
                    at = 0
                    for src, rows, cols in tiles:
                        last = pe.transpose(ps[0:cols, at:at + rows], src, ident[0:rows, 0:rows])
                        at += rows
                    return last
                return run

            pe.wait_ge(w_in, 16 * W_LOADS)
            pe.wait_ge(const_a, 6)
            prep(transposes([(Wk_dup[:, t, :], P, P) for t in range(TILES)]))
            prep(transposes([(Wq_dup[:, t, :], P, P) for t in range(TILES)]))
            prep(transposes([(Wo_sb[:, t * P:(t + 1) * P], C, P) for t in range(TILES)]))
            for k in range(4):
                prep(transposes([(U_sb[:, t, k * P:(k + 1) * P], P, P) for t in range(4)]))
            prep(transposes([(Ur_sb[:, t, :], P, R_INT) for t in range(4)]))

            def wo_wv(half):
                def run(ps):
                    r = slice(half * DH, (half + 1) * DH)
                    for b in range(2):
                        for t in range(TILES):
                            last = pe.matmul(ps[b * C:(b + 1) * C, t * C:(t + 1) * C], Wv_sb[r, t, :], WoT[r, t, :],
                                             start=True, stop=True)
                    return last
                return run

            prep(wo_wv(0), 3)
            prep(wo_wv(1), 3)
            prep(lambda ps: pe.matmul(ps[0:R_INT, :], R_sb[:], BmT[:], start=True, stop=True), 8)

            def w_eff(i):
                def run(ps):
                    for k in range(4):
                        pe.matmul(ps[:], Vh_sb[:, k, i * P:(i + 1) * P], UT[:, k, :], start=(k == 0), stop=False)
                    return pe.matmul(ps[:], Vhr_sb[:, i * P:(i + 1) * P], RBmT[:], start=False, stop=True)
                return run

            for i in range(4):
                prep(w_eff(i), 11)

            def hilo(out_ps, lhs, rhs):
                pass

            def k_front(q, u, par):
                t, b = u // 2, u % 2
                v = U * q + u
                if u == 0:
                    pe.wait_ge(cs_in, 64 * (q + 1))
                wait(pe, k_exp, v)
                for w in (WkT_hi, WkT_lo):
                    last = pe.matmul(ps_kl[:], w[:, t * P:(t + 1) * P], cs[par][:, b, :],
                                     start=(w is WkT_hi), stop=(w is WkT_lo))
                last.then_inc(k_logits, 1)

            def k_back(q, u):
                v = U * q + u
                pe.wait_ge(k_exp, v + 1)
                wait(pe, k_trsb, v)
                for j in range(CHUNKS):
                    last = pe.transpose(ps_kt[:, j * P:(j + 1) * P], ek[u % 2][:, j * P:(j + 1) * P], ident[:])
                last.then_inc(k_tr, 1)

            def k_product(q, t):
                pe.wait_ge(k_trsb, U * q + 2 * t + 2)
                if t == 0:
                    pe.wait_ge(ctx_trsb, q + 1)
                    wait(pe, m_sb, q)
                for j in range(CHUNKS):
                    for b in range(2):
                        last = pe.matmul(ps_m[b * C:(b + 1) * C, t * P:(t + 1) * P], ctxT[:, j, b * C:(b + 1) * C],
                                         ekT[(2 * t + b) % 4][:, j, :], start=(j == 0), stop=(j == CHUNKS - 1))
                last.then_inc(m_done, 1)

            def ctx_transpose(q):
                pe.wait_ge(cin_in, 16 * (q + 1))
                wait(pe, z_lo, q - 2)
                wait(pe, g_sb, 4 * (q - 1))
                for j in range(CHUNKS):
                    last = pe.transpose(ps_x1[:, j * P:(j + 1) * P], cin[:, j * P:(j + 1) * P], ident[:])
                last.then_inc(ctx_tr, 1)

            def g_product(q):
                pe.wait_ge(m_sb, q + 1)
                wait(pe, g_sb, 4 * q)
                wait(pe, y_ok, q - 1)
                pe.wait_ge(ctx_trsb, min(q + 2, PAIRS) if isinstance(q, int) else q + 2)
                for b, ps in ((0, ps_x0), (1, ps_x1)):
                    r = slice(b * C, (b + 1) * C)
                    for t in range(TILES):
                        last = pe.matmul(ps[:, t * P:(t + 1) * P], M_sb[r, t * P:(t + 1) * P],
                                         VO[r, 2 * t:2 * t + 2, :], start=True, stop=True)
                    last.then_inc(g_done, 1)

            def q_front(q, u, par):
                j, b = u // 2, u % 2
                v = U * q + u
                if u == 0:
                    pe.wait_ge(xs_in, 64 * (q + 1))
                wait(pe, q_exp, v)
                for w in (WqT_hi, WqT_lo):
                    last = pe.matmul(ps_ql[:], xs[par][:, b, j * P:(j + 1) * P], w[:],
                                     start=(w is WqT_hi), stop=(w is WqT_lo))
                last.then_inc(q_logits, 1)

            def q_sub(q, u):
                pe.wait_ge(q_max, U * q + u + 1)
                pe.matmul(ps_ql[:], ident_r[:], nm_q[u % 2][:].unsqueeze(2).to_broadcast([P, HEADS, DH]),
                          start=False, stop=True, skip_group_check=True).then_inc(q_shift, 1)

            def q_back(q, u):
                v = U * q + u
                pe.wait_ge(q_norm, v + 1)
                wait(pe, q_trsb, v)
                for t in range(TILES):
                    last = pe.transpose(ps_qt[:, t * P:(t + 1) * P], qn[u % 2][:, 2 * t:2 * t + 2, :], ident[:])
                last.then_inc(q_tr, 1)

            def o_product(q, j):
                pe.wait_ge(q_trsb, U * q + 2 * j + 2)
                if j == 0:
                    pe.wait_ge(g_sb, 4 * (q + 1))
                    wait(pe, o_ok, q)
                for t in range(TILES):
                    for b in range(2):
                        last = pe.matmul(ps_o[b * C:(b + 1) * C, j * P:(j + 1) * P], G_sb[:, b, t, :],
                                         qT[2 * j + b][:, t, :], start=(t == 0), stop=(t == TILES - 1))
                last.then_inc(o_done, 1)

            def ssq(q):
                pe.wait_ge(sq_ok, q + 1)
                if isinstance(q, int) and q == PAIRS - 1:
                    pe.wait_ge(y_ok, q)
                else:
                    pe.wait_ge(g_sb, 4 * (q + 2))
                for j in range(CHUNKS):
                    last = pe.matmul(ps_x0[:, 2 * j:2 * j + 2], o_sq[:, j * P:(j + 1) * P], batch_of[:],
                                     start=True, stop=True)
                last.then_inc(ssq_done, 1)

            def norm_rows(q):
                pe.wait_ge(rn_ok, q + 1)
                for j in range(CHUNKS):
                    for b in range(2):
                        last = pe.matmul(ps_x0[b * C:(b + 1) * C, j * P:(j + 1) * P],
                                         rnorm[:, j, b:b + 1].to_broadcast([P, C]), ident[:], start=True, stop=True)
                last.then_inc(rn_bc, 1)

            def z_transpose(q):
                pe.wait_ge(z_ok, q + 1)
                for i in range(4):
                    last = pe.transpose(ps_x1[:, i * P:(i + 1) * P], x1hat[:, i * P:(i + 1) * P], ident[:])
                last.then_inc(z_tr, 1)

            def ffn(q, half):
                if half == 0:
                    pe.wait_ge(z_lo, q + 1)
                    pe.wait_ge(on_ok, q + 1)
                for i in (2 * half, 2 * half + 1):
                    for z, w in ((zT_hi, Wff_hi), (zT_lo, Wff_hi), (zT_hi, Wff_lo)):
                        last = pe.matmul(ps_x0[:], z[:, i, :], w[:, i, :], start=(i == 0 and z is zT_hi and w is Wff_hi),
                                         stop=(i == 3 and w is Wff_lo))
                if half:
                    last.then_inc(ffn_done, 1)

            def step(p, par, do_k, do_q, do_fin, do_ffn):
                first = isinstance(p, int) and p == -1
                last_k = isinstance(p, int) and p == PAIRS - 1
                prev_q = do_fin
                for u in range(U):
                    if do_k:
                        k_front(p + 1, u, 1 - par)
                    if do_k and u > 0:
                        k_back(p + 1, u - 1)
                    if u == 0 and not first and (do_k or last_k):
                        k_back(p, U - 1)
                    if do_q:
                        q_front(p, u, par)
                    if u == 1:
                        if not first and (do_k or last_k):
                            k_product(p, 3)
                        if do_ffn:
                            ffn(p - 2, 0)
                    if u == 2:
                        if do_ffn:
                            ffn(p - 2, 1)
                        if do_k:
                            ctx_transpose(p + 1)
                    if u in (3, 5, 7) and do_k:
                        k_product(p + 1, (u - 3) // 2)
                    if do_q:
                        q_sub(p, u)
                    if do_q and u > 0:
                        q_back(p, u - 1)
                    if u == 0 and prev_q:
                        q_back(p - 1, U - 1)
                    if u in (1, 3) and prev_q:
                        o_product(p - 1, 2 + u // 2)
                    if u == 3 and do_q:
                        g_product(p)
                    if u == 4 and do_fin:
                        ssq(p - 1)
                    if u in (5, 7) and do_q:
                        o_product(p, (u - 5) // 2)
                    if u == 6 and do_fin:
                        norm_rows(p - 1)
                    if u == 7 and do_fin:
                        z_transpose(p - 1)

            pe.wait_ge(prep_sb, n_prep[0])
            steps(pe, step)

        @block.scalar
        def _(act):
            def k_exponent(q, u, par):
                t, b = u // 2, u % 2
                v = U * q + u
                act.wait_ge(k_max, v + 1)
                wait(act, k_tr, v - 1)
                if u == 0:
                    wait(act, rk_ok, q - 1)
                act.activation(ek[u % 2][:], ps_kl[:], ACT.Exp, bias=nm_k[:, u:u + 1],
                               accum_out=sum_k[par][:, b, t:t + 1]).then_inc(k_exp, 1)

            def k_copy(q, u):
                v = U * q + u
                act.wait_ge(k_tr, v + 1)
                wait(act, m_done, 4 * q + u // 2 - 1)
                act.activation(ekT[u % 4][:], ps_kt[:], ACT.Copy).then_inc(k_trsb, 1)

            def q_exponent(q, u):
                v = U * q + u
                act.wait_ge(q_shift, v + 1)
                wait(act, q_norm, v - 1)
                act.activation(eq[u % 2][:], ps_ql[:], ACT.Exp).then_inc(q_exp, 1)

            def q_copy(q, u):
                v = U * q + u
                act.wait_ge(q_tr, v + 1)
                wait(act, o_done, 4 * (q - 1) + u // 2 + 1)
                act.activation(qT[u][:], ps_qt[:], ACT.Copy).then_inc(q_trsb, 1)

            def step(p, par, do_k, do_q, do_fin, do_ffn):
                first = isinstance(p, int) and p == -1
                last_k = isinstance(p, int) and p == PAIRS - 1
                for u in range(U):
                    if do_k and u > 0:
                        k_copy(p + 1, u - 1)
                    if u == 0 and not first and (do_k or last_k):
                        k_copy(p, U - 1)
                    if do_k:
                        k_exponent(p + 1, u, 1 - par)
                    if do_q:
                        q_exponent(p, u)
                    if do_q and u > 0:
                        q_copy(p, u - 1)
                    if u == 0 and do_fin:
                        q_copy(p - 1, U - 1)
                    if u == 2 and do_k:
                        act.wait_ge(ctx_tr, p + 2)
                        wait(act, m_done, 4 * (p + 1))
                        act.activation(ctxT[:], ps_x1[:], ACT.Copy).then_inc(ctx_trsb, 1)
                    if u == 3 and do_fin:
                        act.wait_ge(o_done, 4 * p)
                        wait(act, on_ok, p - 1)
                        act.activation(o_sb[:], ps_o[:], ACT.Identity, bias=bo_col[:]).then_inc(o_ok, 1)
                    if u == 7 and do_fin:
                        act.wait_ge(z_tr, p)
                        wait(act, ffn_done, p - 1)
                        act.activation(zT_hi[:], ps_x1[:], ACT.Copy).then_inc(z_hi, 1)

            act.wait_ge(w_in, 16 * W_LOADS)
            steps(act, step)

        @block.vector
        def _(dve):
            def c_high(q):
                dve.wait_ge(cin_in, 16 * (q + 1))
                wait(dve, cs_in, 64 * q)
                dve.tensor_copy(c_hi[:], cin[:]).then_inc(c_hi_ok, 1)

            def x_stats(q):
                dve.wait_ge(xin_in, 16 * (q + 1))
                dve.bn_stats(st1[:], xin[:])
                dve.drain()
                dve.bn_aggr(mv1[:], st1[:]).then_inc(x_mv, 1)
                dve.wait_ge(x_mv, q + 1)
                dve.tensor_scalar(var1[:], mv1[:, 1:2], LN_EPS, None, ALU.add).then_inc(x_var, 1)

            def x_normal(q):
                dve.wait_ge(x_rs, q + 1)
                wait(dve, x_lo_ok, q)
                dve.tensor_scalar(xhat[:], xin[:], mv1[:, 0:1], rstd1[:], ALU.subtract, ALU.mult).then_inc(x_hat, 1)

            def x_high(q):
                dve.wait_ge(x_hat, q + 1)
                wait(dve, xs_in, 64 * q)
                dve.tensor_copy(x_hi[:], xhat[:]).then_inc(x_hi_ok, 1)

            c_high(0)

            dve.wait_ge(w_in, 16 * W_LOADS)
            dve.tensor_tensor(head_col[:, 3:4], head_col[:, 0:1], head_col[:, 1:2], ALU.mult).then_inc(prep_col, 1)
            dve.wait_ge(prep_col, 1)
            dve.tensor_tensor(head_col[:, 1:2], head_col[:, 3:4], head_col[:, 2:3], ALU.add).then_inc(prep_col, 1)
            dve.wait_ge(prep_col, 2)
            dve.tensor_scalar(s_col[0:R_TOP, 0:1], head_col[:, 1:2], 0.0, None, ALU.max).then_inc(prep_col, 1)
            dve.tensor_scalar(tail_col[:, 2:3], tail_col[:, 1:2], 0.0, None, ALU.max).then_inc(prep_col, 1)
            dve.wait_ge(prep_col, 4)
            dve.tensor_tensor(tail_col[:, 1:2], tail_col[:, 0:1], tail_col[:, 2:3], ALU.mult).then_inc(prep_col, 1)
            dve.tensor_scalar(g8[:], g_col[:], float(C) ** 0.5, None, ALU.mult).then_inc(prep_col, 1)
            dve.wait_ge(const_a, 4)
            dve.tensor_copy(ident_r[:], ident[:]).then_inc(prep_col, 1)
            dve.wait_ge(prep_col, 7)

            n_prep, n_hi = [0], [0]

            def split(ps, hi, lo):
                dve.tensor_copy(hi, ps).then_inc(prep_hi, 1)
                n_hi[0] += 1
                dve.wait_ge(prep_hi, n_hi[0])
                return dve.tensor_tensor(lo, ps, hi, ALU.subtract)

            def prep(run):
                n = n_prep[0]
                n_prep[0] += 1
                dve.wait_ge(prep_mm, n + 1)
                run(banks[n % len(banks)]).then_inc(prep_sb, 1)

            prep(lambda ps: split(ps[:], WkT_hi[:], WkT_lo[:]))
            prep(lambda ps: split(ps[:], WqT_hi[:], WqT_lo[:]))
            prep(lambda ps: dve.tensor_copy(WoT[:], ps[:, 0:TILES * C].rearrange("p (t o) -> p t o", t=TILES)))
            for k in range(4):
                prep(lambda ps, k=k: dve.tensor_scalar(UT[:, k, :], ps[:], s_col[:, k:k + 1], None, ALU.mult))
            prep(lambda ps: dve.tensor_scalar(BmT[:], ps[0:R_INT, :], tail_col[:, 1:2], None, ALU.mult))
            for half in range(2):
                prep(lambda ps, half=half: dve.tensor_scalar(
                    VO[:].rearrange("p (t s) o -> p t s o", s=2)[:, :, half, :],
                    ps[:, 0:TILES * C].rearrange("p (t o) -> p t o", t=TILES), SCALE, None, ALU.mult))
            prep(lambda ps: dve.tensor_copy(RBmT[:], ps[0:R_INT, :]))
            for i in range(4):
                prep(lambda ps, i=i: split(ps[:], Wff_hi[:, i, :], Wff_lo[:, i, :]))

            def k_maximum(q, u):
                dve.wait_ge(k_logits, U * q + u + 1)
                dve.tensor_reduce(nm_k[:, u:u + 1], ps_kl[:], AX.X, ALU.max, negate=True).then_inc(k_max, 1)

            def q_maximum(q, u):
                dve.wait_ge(q_logits, U * q + u + 1)
                dve.tensor_reduce(nm_q[u % 2][:], ps_ql[:].rearrange("p (h d) -> p h d", h=HEADS), AX.X, ALU.max,
                                  negate=True).then_inc(q_max, 1)

            def q_total(q, u):
                v = U * q + u
                dve.wait_ge(q_exp, v + 1)
                dve.tensor_reduce(sum_q[u % 2][:], eq[u % 2][:], AX.X, ALU.add).then_inc(q_sum, 1)
                dve.wait_ge(q_sum, v + 1)
                dve.reciprocal(rq[u % 2][:], sum_q[u % 2][:]).then_inc(q_rec, 1)

            def step(p, par, do_k, do_q, do_fin, do_ffn):
                first = isinstance(p, int) and p == -1
                for u in range(U):
                    if do_q and u > 0:
                        q_total(p, u - 1)
                    if u == 0 and do_fin:
                        q_total(p - 1, U - 1)
                    if do_k:
                        k_maximum(p + 1, u)
                    if do_q:
                        q_maximum(p, u)
                    if u == 0 and do_k:
                        x_stats(p + 1)
                    if u == 0 and do_ffn:
                        dve.wait_ge(z_hi, p - 1)
                        dve.tensor_tensor(zT_lo[:], ps_x1[:].rearrange("p (i s) -> p i s", i=4), zT_hi[:],
                                          ALU.subtract).then_inc(z_lo, 1)
                    if u == 2 and do_k:
                        x_normal(p + 1)
                        x_high(p + 1)
                    if u == 2 and do_q:
                        dve.wait_ge(m_done, 4 * (p + 1))
                        dve.tensor_copy(M_sb[:], ps_m[:]).then_inc(m_sb, 1)
                        dve.reciprocal(rk[:], sum_k[par][:]).then_inc(rk_ok, 1)
                    if u == 3 and do_ffn:
                        dve.wait_ge(ffn_done, p - 1)
                        dve.wait_ge(x1b_ok, p - 1)
                        wait(dve, y_out, 16 * (p - 2))
                        dve.tensor_tensor(y[:], ps_x0[:], x1b[:], ALU.add).then_inc(y_ok, 1)
                    if u == 4 and do_q:
                        dve.wait_ge(rk_ok, p + 1)
                        wait(dve, o_done, 4 * p)
                        for b, ps in ((0, ps_x0), (1, ps_x1)):
                            dve.wait_ge(g_done, 2 * p + 1 + b)
                            for h in range(2):
                                r = slice(h * DH, (h + 1) * DH)
                                dve.tensor_tensor(
                                    G_sb[r, b, :, :],
                                    ps[:].rearrange("p (t s o) -> p t s o", t=TILES, s=2)[r, :, h, :],
                                    rk[r, b, :].unsqueeze(2).to_broadcast([DH, TILES, C]), ALU.mult).then_inc(g_sb, 1)
                    if u == 5 and do_k and not (isinstance(p, int) and p + 2 >= PAIRS):
                        c_high(p + 2)
                    if u == 5 and do_fin:
                        dve.wait_ge(ssq_done, p)
                        dve.tensor_scalar(ssq_c[:], ps_x0[:, 0:2 * CHUNKS].rearrange("p (j b) -> p j b", b=2),
                                          NORM_EPS ** 2, None, ALU.max).then_inc(ssq_ok, 1)
                    if u == 6 and do_fin:
                        dve.wait_ge(rn_bc, p)
                        dve.tensor_tensor(on[:], ps_x0[:], o_sb[:], ALU.mult).then_inc(on_ok, 1)
                        dve.wait_ge(on_ok, p)
                        dve.wait_ge(xres_in, 16 * p)
                        wait(dve, x1b_ok, p - 1)
                        dve.scalar_tensor_tensor(out=x1[:], in0=on[:], scalar=g8[:], in1=xres[:], op0=ALU.mult,
                                                 op1=ALU.add).then_inc(x1_ok, 1)
                        dve.wait_ge(x1_ok, p)
                        dve.bn_stats(st2[:], x1[:])
                        dve.drain()
                        dve.bn_aggr(mv2[:], st2[:]).then_inc(z_mv, 1)
                        dve.wait_ge(z_mv, p)
                        dve.tensor_scalar(var2[:], mv2[:, 1:2], LN_EPS, None, ALU.add).then_inc(z_var, 1)
                    if u == 7 and do_fin:
                        dve.wait_ge(z_rs, p)
                        dve.tensor_scalar(x1hat[:], x1[:], mv2[:, 0:1], rstd2[:], ALU.subtract, ALU.mult)\
                           .then_inc(z_ok, 1)

            steps(dve, step)


_INS = ['x', 'ctx_4096', 'L0_xattn_Wq', 'L0_xattn_Wk', 'L0_xattn_Wv', 'L0_xattn_Wo', 'L0_xattn_bo', 'L0_xattn_g',
        'L0_ffn_U_top', 'L0_ffn_S_top', 'L0_ffn_Vh_top', 'L0_ffn_U_tail', 'L0_ffn_S_tail', 'L0_ffn_Vh_tail',
        'L0_ffn_U_tail_r', 'L0_ffn_S_tail_r', 'L0_ffn_Vh_tail_r', 'L0_ffn_alpha', 'L0_ffn_beta', 'L0_ffn_D',
        'L0_ffn_R', 'L0_ffn_bias']
_OUTS = [((32, 64, 512), 'float32')]


def kernel(**inputs):
    import numpy as _np
    import concourse.bacc as _bacc
    from concourse import mybir as _mybir
    from concourse.bass_utils import run_bass_kernel_spmd as _run

    nc = _bacc.Bacc("TRN2", target_bir_lowering=False, num_devices=1)
    arrays, args = {}, []
    for name in _INS:
        a = _np.ascontiguousarray(inputs[name])
        arrays[f"in_{name}_dram"] = a
        args.append(nc.dram_tensor(f"in_{name}_dram", a.shape, _mybir.dt.from_np(a.dtype), kind="ExternalInput").ap())
    for i, (shape, dtype) in enumerate(_OUTS):
        dt = _mybir.dt.from_np(_np.dtype(dtype))
        args.append(nc.dram_tensor(f"out_{i}_dram", shape, dt, kind="ExternalOutput").ap())
    xattn_ffn(nc, *args)
    r = _run(nc, [arrays], core_ids=[0])
    got = tuple(r.results[0][f"out_{i}_dram"] for i in range(len(_OUTS)))
    return got[0]
```

```python
from contextlib import ExitStack

import concourse.bass as bass
from concourse import mybir

ALU = mybir.AluOpType
ACT = mybir.ActivationFunctionType
AX = mybir.AxisListType
F32 = mybir.dt.float32
F32R = mybir.dt.float32r

P = 128
BATCH, C, N = 32, 64, 512
HEADS, DH = 8, 64
HID = HEADS * DH
PAIRS = BATCH // 2
TILES = HID // P
CHUNKS = N // P
U = 2 * TILES
R_TOP, R_INT = 64, 4
R_TAIL = N - R_TOP
SCALE = float(DH) ** -0.5
LN_EPS = 1e-5
NORM_EPS = 1e-12
BANK = 512
N_PREP = 15


def xattn_ffn(nc, x, ctx, Wq, Wk, Wv, Wo, bo, g, U_top, S_top, Vh_top, U_tail, S_tail, Vh_tail,
              U_tail_r, S_tail_r, Vh_tail_r, alpha, beta, D, R, bias, out):
    es = ExitStack()
    with es:
        def sb(name, shape, dt=F32):
            return es.enter_context(nc.sbuf_tensor(name, shape, dt))

        def sem(name):
            return es.enter_context(nc.semaphore(name))

        def bank(name):
            return es.enter_context(nc.psum_tensor(name, [P, BANK], F32))

        ps_kl = bank("ps_kl")
        ps_ql = bank("ps_ql")
        ps_kt = bank("ps_kt")
        ps_qt = bank("ps_qt")
        ps_m = bank("ps_m")
        ps_o = bank("ps_o")
        ps_x0 = bank("ps_x0")
        ps_x1 = bank("ps_x1")
        prep_banks = [ps_o, ps_ql, ps_qt, ps_x0]

        ident = sb("ident", [P, P])
        ident_r = sb("ident_r", [P, P], F32R)
        batch_of = sb("batch_of", [P, 2])
        minus_half = sb("minus_half", [P, 2 * CHUNKS])
        U_sb = sb("U_sb", [P, 4, N])
        Ur_sb = sb("Ur_sb", [P, 4, R_INT])
        UT = sb("UT", [P, 4, N])
        Vh_sb = sb("Vh_sb", [P, 4, N])
        Vhr_sb = sb("Vhr_sb", [R_INT, N])
        R_sb = sb("R_sb", [R_INT, R_INT])
        s_col = sb("s_col", [P, 4])
        head_col = sb("head_col", [R_TOP, 4])
        tail_col = sb("tail_col", [R_INT, 3])
        BmT = sb("BmT", [R_INT, N])
        RBmT = sb("RBmT", [R_INT, N])
        Wff_hi = sb("Wff_hi", [P, 4, N], F32R)
        Wff_lo = sb("Wff_lo", [P, 4, N], F32R)
        Wq_dup = sb("Wq_dup", [P, TILES, 2 * C])
        Wk_dup = sb("Wk_dup", [P, TILES, 2 * C])
        WqT_hi = sb("WqT_hi", [P, HID], F32R)
        WqT_lo = sb("WqT_lo", [P, HID], F32R)
        WkT_hi = sb("WkT_hi", [P, HID], F32R)
        WkT_lo = sb("WkT_lo", [P, HID], F32R)
        Wv_sb = sb("Wv_sb", [P, TILES, C])
        Wo_sb = sb("Wo_sb", [C, HID])
        WoT = sb("WoT", [P, TILES, C])
        VO = sb("VO", [P, HEADS, 2, C])
        g_col = sb("g_col", [P, 1])
        g8 = sb("g8", [P, 1])
        bo_col = sb("bo_col", [P, 1])
        bias_bc = sb("bias_bc", [P, N])

        xin = sb("xin", [P, N])
        cin = sb("cin", [P, N])
        xres = sb("xres", [P, N])
        xhat = sb("xhat", [P, N])
        x_hi = sb("x_hi", [P, N], F32R)
        x_lo = sb("x_lo", [P, N], F32R)
        c_hi = sb("c_hi", [P, N], F32R)
        c_lo = sb("c_lo", [P, N], F32R)
        xs = [sb(f"xs{i}", [P, 2, N], F32R) for i in range(2)]
        cs = [sb(f"cs{i}", [P, 2, N], F32R) for i in range(2)]
        ctxT = [sb(f"ctxT{i}", [P, CHUNKS, P]) for i in range(2)]
        st1 = sb("st1", [P, 6])
        mv1 = sb("mv1", [P, 2])
        var1 = sb("var1", [P, 1])
        rstd1 = sb("rstd1", [P, 1])
        nm_k = sb("nm_k", [P, U])
        sum_k = [sb(f"sum_k{i}", [P, TILES, 2]) for i in range(2)]
        rk = sb("rk", [P, TILES, 2])
        ek = [sb(f"ek{i}", [P, N]) for i in range(2)]
        ekT = [sb(f"ekT{i}", [P, CHUNKS, P]) for i in range(4)]
        nm_q = [sb(f"nm_q{i}", [P, HEADS], F32R) for i in range(2)]
        eq = [sb(f"eq{i}", [P, HEADS, DH]) for i in range(4)]
        sum_q = [sb(f"sum_q{i}", [P, HEADS]) for i in range(4)]
        rq = [sb(f"rq{i}", [P, HEADS]) for i in range(4)]
        qn = [sb(f"qn{i}", [P, HEADS, DH]) for i in range(4)]
        qT = [sb(f"qT{i}", [P, TILES, P]) for i in range(8)]
        M_sb = sb("M_sb", [P, HID])
        G_sb = [sb(f"G_sb{i}", [P, TILES, 2, C]) for i in range(2)]
        o_sb = sb("o_sb", [P, N])
        o_sq = sb("o_sq", [P, N])
        ssq_c = sb("ssq_c", [P, CHUNKS, 2])
        rnorm = sb("rnorm", [P, CHUNKS, 2])
        on_sb = sb("on_sb", [P, N])
        x1 = sb("x1", [P, N])
        x1b = sb("x1b", [P, N])
        st2 = sb("st2", [P, 6])
        mv2 = sb("mv2", [P, 2])
        var2 = sb("var2", [P, 1])
        rstd2 = sb("rstd2", [P, 1])
        x1hat = sb("x1hat", [P, N])
        zT_hi = sb("zT_hi", [P, 4, P], F32R)
        zT_lo = sb("zT_lo", [P, 4, P], F32R)
        y = sb("y", [P, N])

        wk_in = sem("wk_in")
        w_in = sem("w_in")
        const_a = sem("const_a")
        prep_col = sem("prep_col")
        prep_mm = sem("prep_mm")
        prep_sb = sem("prep_sb")
        prep_hi = sem("prep_hi")
        xin_in, cin_in, xres_in = sem("xin_in"), sem("cin_in"), sem("xres_in")
        x_mv, x_var, x_rs, x_hat = sem("x_mv"), sem("x_var"), sem("x_rs"), sem("x_hat")
        x_hi_ok, x_lo_ok, c_hi_ok, c_lo_ok = sem("x_hi_ok"), sem("x_lo_ok"), sem("c_hi_ok"), sem("c_lo_ok")
        xs_in, cs_in = sem("xs_in"), sem("cs_in")
        k_logits, k_max, k_exp = sem("k_logits"), sem("k_max"), sem("k_exp")
        k_tr, k_trsb = sem("k_tr"), sem("k_trsb")
        ctx_tr, ctx_trsb = sem("ctx_tr"), sem("ctx_trsb")
        m_done, m_sb, rk_ok = sem("m_done"), sem("m_sb"), sem("rk_ok")
        g_done, g_sb = sem("g_done"), sem("g_sb")
        q_logits, q_max, q_shift, q_exp = sem("q_logits"), sem("q_max"), sem("q_shift"), sem("q_exp")
        q_sum, q_rec, q_norm, q_tr, q_trsb = sem("q_sum"), sem("q_rec"), sem("q_norm"), sem("q_tr"), sem("q_trsb")
        o_done, o_ok, sq_ok, ssq_done = sem("o_done"), sem("o_ok"), sem("sq_ok"), sem("ssq_done")
        ssq_ok, rn_ok, rn_bc = sem("ssq_ok"), sem("rn_ok"), sem("rn_bc")
        on_ok, x1_ok, x1b_ok = sem("on_ok"), sem("x1_ok"), sem("x1b_ok")
        z_mv, z_var, z_rs, z_ok = sem("z_mv"), sem("z_var"), sem("z_rs"), sem("z_ok")
        z_tr, z_hi, z_lo = sem("z_tr"), sem("z_hi"), sem("z_lo")
        ffn_done, y_ok, y_out = sem("ffn_done"), sem("y_ok"), sem("y_out")

        x_d = x.rearrange("(q b) c n -> q (b c) n", b=2)
        ctx_d = ctx.rearrange("(q b) c n -> q (b c) n", b=2)
        out_d = out.rearrange("(q b) c n -> q (b c) n", b=2)

        def wait(eng, s, value):
            if isinstance(value, int) and value <= 0:
                return
            eng.wait_ge(s, value)

        def upto(count, last=PAIRS):
            return min(count, last) if isinstance(count, int) else count

        def on(q):
            return not isinstance(q, int) or 0 <= q < PAIRS

        def steps(eng, step):
            for p in range(-1, 3):
                step(p, p % 2)
            with eng.Fori(1, PAIRS // 2 - 2) as i:
                step(2 * i + 1, 1)
                step(2 * i + 2, 0)
            for p in range(PAIRS - 3, PAIRS + 3):
                step(p, p % 2)

        block = es.enter_context(nc.Block())

        W_LOADS = 0

        @block.sync
        def _(sp):
            nonlocal W_LOADS

            def load(dst, src):
                nonlocal W_LOADS
                sp.dma_start(dst, src).then_inc(w_in, 16)
                W_LOADS += 1

            def load_pair(dst, src, s):
                sp.dma_start(dst, src).then_inc(s, 16)

            def col(v):
                return v.rearrange("(n a) -> n a", a=1)

            def load_cin(q):
                wait(sp, c_lo_ok, q)
                wait(sp, c_hi_ok, q)
                wait(sp, ctx_tr, q)
                sp.dma_start(cin[:], ctx_d[q]).then_inc(cin_in, 16)

            def load_xin(q):
                wait(sp, x_hat, q)
                sp.dma_start(xin[:], x_d[q]).then_inc(xin_in, 16)

            def stack(q, par, hi, lo, hi_ok, lo_ok, dst, landed):
                wait(sp, hi_ok, q + 1)
                wait(sp, lo_ok, q + 1)
                for b in range(2):
                    sp.dma_start(dst[par][0:C, b, :].bitcast(F32), hi[b * C:(b + 1) * C, :].bitcast(F32)).then_inc(landed, 16)
                    sp.dma_start(dst[par][C:P, b, :].bitcast(F32), lo[b * C:(b + 1) * C, :].bitcast(F32)).then_inc(landed, 16)

            sp.dma_start(cin[:], ctx_d[0]).then_inc(cin_in, 16)
            for d in range(2):
                sp.dma_start(Wk_dup[:, :, d * C:(d + 1) * C], Wk.rearrange("(t p) c -> p t c", p=P)).then_inc(wk_in, 16)
            stack(0, 0, c_hi, c_lo, c_hi_ok, c_lo_ok, cs, cs_in)
            sp.dma_start(xin[:], x_d[0]).then_inc(xin_in, 16)
            for d in range(2):
                load(Wq_dup[:, :, d * C:(d + 1) * C], Wq.rearrange("(t p) c -> p t c", p=P))
            load(Wv_sb[:], Wv.rearrange("(t p) c -> p t c", p=P))
            load(Wo_sb[:], Wo)
            for b in range(2):
                load(bo_col[b * C:(b + 1) * C, :], col(bo))
                load(g_col[b * C:(b + 1) * C, :], g[0])
            load(U_sb[:, :, 0:R_TOP], U_top.rearrange("(t p) r -> p t r", p=P))
            load(U_sb[:, :, R_TOP:N], U_tail.rearrange("(t p) r -> p t r", p=P))
            load(Ur_sb[:], U_tail_r.rearrange("(t p) r -> p t r", p=P))
            load(Vh_sb[0:R_TOP, 0, :], Vh_top)
            load(Vh_sb[R_TOP:P, 0, :], Vh_tail[0:P - R_TOP, :])
            load(Vh_sb[:, 1:4, :], Vh_tail[P - R_TOP:R_TAIL, :].rearrange("(t p) i -> p t i", p=P))
            load(Vhr_sb[:], Vh_tail_r)
            load(R_sb[:], R)
            load(head_col[:, 0:1], col(S_top))
            load(head_col[:, 1:2], col(alpha))
            load(head_col[:, 2:3], col(beta))
            load(tail_col[:, 0:1], col(S_tail_r))
            load(tail_col[:, 1:2], col(D))
            load(s_col[R_TOP:P, 0:1], col(S_tail[0:P - R_TOP]))
            for t in range(1, 4):
                a = P - R_TOP + (t - 1) * P
                load(s_col[:, t:t + 1], col(S_tail[a:a + P]))
            load(bias_bc[:], bias.rearrange("(a n) -> a n", a=1).to_broadcast([P, N]))

            def step(p, par):
                if on(p + 2):
                    load_cin(p + 2)
                    load_xin(p + 2)
                if on(p + 1):
                    stack(p + 1, 1 - par, x_hi, x_lo, x_hi_ok, x_lo_ok, xs, xs_in)
                if on(p + 2):
                    stack(p + 2, par, c_hi, c_lo, c_hi_ok, c_lo_ok, cs, cs_in)
                if on(p - 3):
                    wait(sp, y_ok, p - 2)
                    sp.dma_start(out_d[p - 3], y[:]).then_inc(y_out, 16)
                if on(p - 1):
                    wait(sp, x1_ok, p - 1)
                    sp.dma_start(xres[:], x_d[p - 1]).then_inc(xres_in, 16)

            steps(sp, step)
            sp.wait_ge(y_out, 16 * PAIRS)

        @block.gpsimd
        def _(pool):
            pool.memset(ident[:], 0.0).then_inc(const_a, 1)
            pool.memset(batch_of[:], 0.0).then_inc(const_a, 1)
            pool.memset(minus_half[:], -0.5).then_inc(const_a, 1)
            pool.wait_ge(const_a, 3)
            pool.affine_select(out=ident[:], in_=ident[:], compare_op=ALU.not_equal, fill=1.0, base=0,
                               pattern=[[-1, P]], channel_multiplier=1).then_inc(const_a, 1)
            for b in range(2):
                pool.wait_ge(const_a, 4 + b)
                pool.memset(batch_of[b * C:(b + 1) * C, b:b + 1], 1.0).then_inc(const_a, 1)
            pool.wait_ge(const_a, 6)

            def c_low(q):
                pool.wait_ge(c_hi_ok, q + 1)
                wait(pool, cs_in, 64 * q)
                pool.tensor_tensor(c_lo[:], cin[:], c_hi[:], ALU.subtract).then_inc(c_lo_ok, 1)

            def x_low(q):
                pool.wait_ge(x_hi_ok, q + 1)
                wait(pool, xs_in, 64 * q)
                pool.tensor_tensor(x_lo[:], xhat[:], x_hi[:], ALU.subtract).then_inc(x_lo_ok, 1)

            c_low(0)

            def x_rstd(q):
                pool.wait_ge(x_var, q + 1)
                pool.tensor_tensor(rstd1[:], var1[:], minus_half[:, 0:1], ALU.pow).then_inc(x_rs, 1)

            def norm(q, u):
                v = U * q + u
                pool.wait_ge(q_rec, v + 1)
                wait(pool, q_tr, v - 3)
                pool.tensor_tensor(qn[u % 4][:], eq[u % 4][:], rq[u % 4][:].unsqueeze(2).to_broadcast([P, HEADS, DH]),
                                   ALU.mult).then_inc(q_norm, 1)

            def step(p, par):
                q_fin = p - 2
                for u in range(U):
                    if u > 0 and on(p):
                        norm(p, u - 1)
                    if u == 0 and on(p - 1):
                        norm(p - 1, U - 1)
                    if u == 0 and on(p + 1):
                        x_rstd(p + 1)
                    if u == 1 and on(q_fin):
                        pool.wait_ge(ssq_ok, q_fin + 1)
                        pool.tensor_tensor(rnorm[:], ssq_c[:], minus_half[:].rearrange("p (j b) -> p j b", b=2),
                                           ALU.pow).then_inc(rn_ok, 1)
                    if u == 2 and on(p + 1):
                        x_low(p + 1)
                    if u == 3 and on(p + 2):
                        c_low(p + 2)
                    if u == 4 and on(q_fin):
                        pool.wait_ge(z_var, q_fin + 1)
                        pool.tensor_tensor(rstd2[:], var2[:], minus_half[:, 0:1], ALU.pow).then_inc(z_rs, 1)
                    if u == 6 and on(q_fin):
                        pool.wait_ge(x1_ok, q_fin + 1)
                        wait(pool, y_ok, q_fin)
                        pool.tensor_tensor(x1b[:], x1[:], bias_bc[:], ALU.add).then_inc(x1b_ok, 1)
                    if u == 7 and on(p - 1):
                        pool.wait_ge(o_ok, p)
                        wait(pool, ssq_done, p - 1)
                        pool.tensor_tensor(o_sq[:], o_sb[:], o_sb[:], ALU.mult).then_inc(sq_ok, 1)

            pool.wait_ge(w_in, 16 * W_LOADS)
            steps(pool, step)

        @block.tensor
        def _(pe):
            n_prep = [0]

            def prep(run, needs=0):
                n = n_prep[0]
                n_prep[0] += 1
                wait(pe, prep_sb, max(needs, n - len(prep_banks) + 1))
                run(prep_banks[n % len(prep_banks)]).then_inc(prep_mm, 1)

            def transposes(tiles):
                def run(ps):
                    at = 0
                    for src, rows, cols in tiles:
                        last = pe.transpose(ps[0:cols, at:at + rows], src, ident[0:rows, 0:rows])
                        at += rows
                    return last
                return run

            def wo_wv(half):
                def run(ps):
                    r = slice(half * DH, (half + 1) * DH)
                    for b in range(2):
                        for t in range(TILES):
                            last = pe.matmul(ps[b * C:(b + 1) * C, t * C:(t + 1) * C], Wv_sb[r, t, :], WoT[r, t, :],
                                             start=True, stop=True)
                    return last
                return run

            def w_eff(i):
                def run(ps):
                    for k in range(4):
                        pe.matmul(ps[:], Vh_sb[:, k, i * P:(i + 1) * P], UT[:, k, :], start=(k == 0), stop=False)
                    return pe.matmul(ps[:], Vhr_sb[:, i * P:(i + 1) * P], RBmT[:], start=False, stop=True)
                return run

            prep_runs = [
                (transposes([(Wk_dup[:, t, :], P, P) for t in range(TILES)]), 0),
                (transposes([(Wq_dup[:, t, :], P, P) for t in range(TILES)]), 0),
                (transposes([(Wo_sb[:, t * P:(t + 1) * P], C, P) for t in range(TILES)]), 0),
                *[(transposes([(U_sb[:, t, k * P:(k + 1) * P], P, P) for t in range(4)]), 0) for k in range(4)],
                (transposes([(Ur_sb[:, t, :], P, R_INT) for t in range(4)]), 0),
                (wo_wv(0), 3),
                (wo_wv(1), 3),
                (lambda ps: pe.matmul(ps[0:R_INT, :], R_sb[:], BmT[:], start=True, stop=True), 8),
                *[(w_eff(i), 11) for i in range(4)],
            ]
            assert len(prep_runs) == N_PREP
            pe.wait_ge(wk_in, 32)
            pe.wait_ge(const_a, 6)
            prep(*prep_runs[0])
            pe.wait_ge(prep_sb, 1)

            def k_front(q, u, par):
                t, b = u // 2, u % 2
                v = U * q + u
                if u == 0:
                    pe.wait_ge(cs_in, 64 * (q + 1))
                wait(pe, k_exp, v)
                for w in (WkT_hi, WkT_lo):
                    last = pe.matmul(ps_kl[:], w[:, t * P:(t + 1) * P], cs[par][:, b, :],
                                     start=(w is WkT_hi), stop=(w is WkT_lo))
                last.then_inc(k_logits, 1)

            def k_back(q, u):
                v = U * q + u
                pe.wait_ge(k_exp, v + 1)
                wait(pe, k_trsb, v)
                for j in range(CHUNKS):
                    last = pe.transpose(ps_kt[:, j * P:(j + 1) * P], ek[u % 2][:, j * P:(j + 1) * P], ident[:])
                last.then_inc(k_tr, 1)

            def k_product(q, t, half, par):
                if half == 0:
                    pe.wait_ge(k_trsb, U * q + 2 * t + 2)
                    if t == 0:
                        pe.wait_ge(ctx_trsb, q + 1)
                        wait(pe, m_sb, q)
                for j in (2 * half, 2 * half + 1):
                    for b in range(2):
                        last = pe.matmul(ps_m[b * C:(b + 1) * C, t * P:(t + 1) * P],
                                         ctxT[par][:, j, b * C:(b + 1) * C], ekT[(2 * t + b) % 4][:, j, :],
                                         start=(j == 0), stop=(j == CHUNKS - 1))
                if half:
                    last.then_inc(m_done, 1)

            def ctx_transpose(q):
                pe.wait_ge(cin_in, 16 * (q + 1))
                wait(pe, z_lo, q - 3)
                wait(pe, ctx_trsb, q)
                for j in range(CHUNKS):
                    last = pe.transpose(ps_x1[:, j * P:(j + 1) * P], cin[:, j * P:(j + 1) * P], ident[:])
                last.then_inc(ctx_tr, 1)

            def g_product(q):
                pe.wait_ge(m_sb, q + 1)
                wait(pe, g_sb, q)
                wait(pe, y_ok, q - 2)
                for t in range(TILES):
                    for s in range(2):
                        at = t * P + s * DH
                        last = pe.matmul(ps_x0[s * DH:(s + 1) * DH, t * P:(t + 1) * P], M_sb[:, at:at + DH],
                                         VO[:, 2 * t + s, :, :], start=True, stop=True)
                last.then_inc(g_done, 1)

            def q_front(q, u, par):
                j, b = u // 2, u % 2
                v = U * q + u
                if u == 0:
                    pe.wait_ge(xs_in, 64 * (q + 1))
                wait(pe, q_exp, v)
                for w in (WqT_hi, WqT_lo):
                    last = pe.matmul(ps_ql[:], xs[par][:, b, j * P:(j + 1) * P], w[:],
                                     start=(w is WqT_hi), stop=(w is WqT_lo))
                last.then_inc(q_logits, 1)

            def q_sub(q, u):
                pe.wait_ge(q_max, U * q + u + 1)
                pe.matmul(ps_ql[:], ident_r[:], nm_q[u % 2][:].unsqueeze(2).to_broadcast([P, HEADS, DH]),
                          start=False, stop=True, skip_group_check=True).then_inc(q_shift, 1)

            def q_back(q, u):
                v = U * q + u
                pe.wait_ge(q_norm, v + 1)
                wait(pe, q_trsb, v)
                for t in range(TILES):
                    last = pe.transpose(ps_qt[:, t * P:(t + 1) * P], qn[u % 4][:, 2 * t:2 * t + 2, :], ident[:])
                last.then_inc(q_tr, 1)

            def o_product(q, j, half, par):
                if half == 0:
                    pe.wait_ge(q_trsb, U * q + 2 * j + 2)
                    if j == 0:
                        pe.wait_ge(g_sb, q + 1)
                        wait(pe, o_ok, q)
                for t in (2 * half, 2 * half + 1):
                    for b in range(2):
                        last = pe.matmul(ps_o[b * C:(b + 1) * C, j * P:(j + 1) * P], G_sb[par][:, t, b, :],
                                         qT[2 * j + b][:, t, :], start=(t == 0), stop=(t == TILES - 1))
                if half:
                    last.then_inc(o_done, 1)

            def ssq(q):
                pe.wait_ge(sq_ok, q + 1)
                pe.wait_ge(ctx_trsb, upto(q + 4))
                wait(pe, z_lo, q)
                for j in range(CHUNKS):
                    last = pe.matmul(ps_x1[:, 2 * j:2 * j + 2], o_sq[:, j * P:(j + 1) * P], batch_of[:],
                                     start=True, stop=True)
                last.then_inc(ssq_done, 1)

            def norm_rows(q):
                pe.wait_ge(rn_ok, q + 1)
                for j in range(CHUNKS):
                    for b in range(2):
                        last = pe.matmul(ps_x1[b * C:(b + 1) * C, j * P:(j + 1) * P],
                                         rnorm[:, j, b:b + 1].to_broadcast([P, C]), ident[:], start=True, stop=True)
                last.then_inc(rn_bc, 1)

            def z_transpose(q):
                pe.wait_ge(z_ok, q + 1)
                for i in range(4):
                    last = pe.transpose(ps_x1[:, i * P:(i + 1) * P], x1hat[:, i * P:(i + 1) * P], ident[:])
                last.then_inc(z_tr, 1)

            def ffn(q, half):
                if half == 0:
                    pe.wait_ge(z_lo, q + 1)
                    pe.wait_ge(g_sb, upto(q + 3))
                    wait(pe, y_ok, q)
                for i in (2 * half, 2 * half + 1):
                    for z, w in ((zT_hi, Wff_hi), (zT_lo, Wff_hi), (zT_hi, Wff_lo)):
                        last = pe.matmul(ps_x0[:], z[:, i, :], w[:, i, :], start=(i == 0 and z is zT_hi and w is Wff_hi),
                                         stop=(i == 3 and w is Wff_lo))
                if half:
                    last.then_inc(ffn_done, 1)

            def step(p, par):
                for u in range(U):
                    if u == 1 and on(p - 2):
                        ssq(p - 2)
                    if on(p):
                        q_front(p, u, par)
                    if on(p + 1):
                        k_front(p + 1, u, 1 - par)
                    if u > 0 and on(p + 1):
                        k_back(p + 1, u - 1)
                    if u == 0 and on(p):
                        k_back(p, U - 1)
                    if u == 0 and on(p + 1):
                        ctx_transpose(p + 1)
                    if on(p):
                        q_sub(p, u)
                    if u >= 3 and on(p + 1):
                        k_product(p + 1, (u - 3) // 2, (u - 3) % 2, 1 - par)
                    if u < 3 and on(p):
                        k_product(p, (u + 5) // 2, (u + 5) % 2, par)
                    if u == 6 and on(p - 2):
                        z_transpose(p - 2)
                    if u > 1 and on(p):
                        q_back(p, u - 2)
                    if u < 2 and on(p - 1):
                        q_back(p - 1, U - 2 + u)
                    if u in (1, 2) and on(p - 3):
                        ffn(p - 3, u - 1)
                    if u == 4 and on(p):
                        g_product(p)
                    if u == 7 and on(p):
                        o_product(p, 0, 0, par)
                    if u < 7 and on(p - 1):
                        o_product(p - 1, (u + 1) // 2, (u + 1) % 2, 1 - par)
                    if u == 2 and on(p - 2):
                        norm_rows(p - 2)
                    if isinstance(p, int) and p == -1:
                        if u == 0:
                            pe.wait_ge(w_in, 16 * W_LOADS)
                        for n in range(2 * u + 1, min(2 * u + 3, N_PREP)):
                            prep(*prep_runs[n])
                if isinstance(p, int) and p == -1:
                    pe.wait_ge(prep_sb, N_PREP)

            steps(pe, step)

        @block.scalar
        def _(act):
            def k_exponent(q, u, par):
                t, b = u // 2, u % 2
                v = U * q + u
                act.wait_ge(k_max, v + 1)
                wait(act, k_tr, v - 1)
                if u == 0:
                    wait(act, rk_ok, q - 1)
                act.activation(ek[u % 2][:], ps_kl[:], ACT.Exp, bias=nm_k[:, u:u + 1],
                               accum_out=sum_k[par][:, t, b:b + 1]).then_inc(k_exp, 1)

            def k_copy(q, u):
                v = U * q + u
                act.wait_ge(k_tr, v + 1)
                wait(act, m_done, 4 * q + u // 2 - 1)
                act.activation(ekT[u % 4][:], ps_kt[:], ACT.Copy).then_inc(k_trsb, 1)

            def q_exponent(q, u):
                v = U * q + u
                act.wait_ge(q_shift, v + 1)
                wait(act, q_norm, v - 3)
                act.activation(eq[u % 4][:], ps_ql[:], ACT.Exp).then_inc(q_exp, 1)

            def q_copy(q, u):
                v = U * q + u
                act.wait_ge(q_tr, v + 1)
                wait(act, o_done, 4 * (q - 1) + u // 2 + 1)
                act.activation(qT[u][:], ps_qt[:], ACT.Copy).then_inc(q_trsb, 1)

            def step(p, par):
                for u in range(U):
                    if u == 7 and on(p - 1):
                        act.wait_ge(o_done, 4 * p)
                        wait(act, on_ok, p - 1)
                        wait(act, sq_ok, p - 1)
                        act.activation(o_sb[:], ps_o[:], ACT.Identity, bias=bo_col[:]).then_inc(o_ok, 1)
                    if u > 0 and on(p + 1):
                        k_copy(p + 1, u - 1)
                    if u == 0 and on(p):
                        k_copy(p, U - 1)
                    if u == 0 and on(p + 1):
                        act.wait_ge(ctx_tr, p + 2)
                        wait(act, m_done, 4 * p)
                        act.activation(ctxT[1 - par][:], ps_x1[:], ACT.Copy).then_inc(ctx_trsb, 1)
                    if on(p + 1):
                        k_exponent(p + 1, u, 1 - par)
                    if on(p):
                        q_exponent(p, u)
                    if u > 1 and on(p):
                        q_copy(p, u - 2)
                    if u < 2 and on(p - 1):
                        q_copy(p - 1, U - 2 + u)
                    if u == 6 and on(p - 2):
                        act.wait_ge(z_tr, p - 1)
                        wait(act, ffn_done, p - 2)
                        act.activation(zT_hi[:], ps_x1[:], ACT.Copy).then_inc(z_hi, 1)
                if isinstance(p, int) and p == -1:
                    act.wait_ge(w_in, 16 * W_LOADS)

            steps(act, step)

        @block.vector
        def _(dve):
            def c_high(q):
                dve.wait_ge(cin_in, 16 * (q + 1))
                wait(dve, cs_in, 64 * q)
                dve.tensor_copy(c_hi[:], cin[:]).then_inc(c_hi_ok, 1)

            def x_stats(q):
                dve.wait_ge(xin_in, 16 * (q + 1))
                dve.bn_stats(st1[:], xin[:])
                dve.drain()
                dve.bn_aggr(mv1[:], st1[:]).then_inc(x_mv, 1)
                dve.wait_ge(x_mv, q + 1)
                dve.tensor_scalar(var1[:], mv1[:, 1:2], LN_EPS, None, ALU.add).then_inc(x_var, 1)

            def x_normal(q):
                dve.wait_ge(x_rs, q + 1)
                wait(dve, x_lo_ok, q)
                dve.tensor_scalar(xhat[:], xin[:], mv1[:, 0:1], rstd1[:], ALU.subtract, ALU.mult).then_inc(x_hat, 1)

            def x_high(q):
                dve.wait_ge(x_hat, q + 1)
                wait(dve, xs_in, 64 * q)
                dve.tensor_copy(x_hi[:], xhat[:]).then_inc(x_hi_ok, 1)

            n_hi = [0]

            def split(ps, hi, lo):
                dve.tensor_copy(hi, ps).then_inc(prep_hi, 1)
                n_hi[0] += 1
                dve.wait_ge(prep_hi, n_hi[0])
                return dve.tensor_tensor(lo, ps, hi, ALU.subtract)

            n_prep = [0]

            def prep(run):
                n = n_prep[0]
                n_prep[0] += 1
                dve.wait_ge(prep_mm, n + 1)
                run(prep_banks[n % len(prep_banks)]).then_inc(prep_sb, 1)

            def vo_block(ps, half):
                for b in range(2):
                    r = slice(b * C, (b + 1) * C)
                    last = dve.tensor_scalar(VO[:].rearrange("p (t s) a o -> p t s a o", s=2)[r, :, half, b, :],
                                             ps[r, 0:TILES * C].rearrange("p (t o) -> p t o", t=TILES),
                                             SCALE, None, ALU.mult)
                return last

            prep_runs = [
                lambda ps: split(ps[:], WkT_hi[:], WkT_lo[:]),
                lambda ps: split(ps[:], WqT_hi[:], WqT_lo[:]),
                lambda ps: dve.tensor_copy(WoT[:], ps[:, 0:TILES * C].rearrange("p (t o) -> p t o", t=TILES)),
                *[lambda ps, k=k: dve.tensor_scalar(UT[:, k, :], ps[:], s_col[:, k:k + 1], None, ALU.mult)
                  for k in range(4)],
                lambda ps: dve.tensor_scalar(BmT[:], ps[0:R_INT, :], tail_col[:, 1:2], None, ALU.mult),
                lambda ps: vo_block(ps, 0),
                lambda ps: vo_block(ps, 1),
                lambda ps: dve.tensor_copy(RBmT[:], ps[0:R_INT, :]),
                *[lambda ps, i=i: split(ps[:], Wff_hi[:, i, :], Wff_lo[:, i, :]) for i in range(4)],
            ]

            def scale_columns():
                dve.wait_ge(w_in, 16 * W_LOADS)
                dve.tensor_tensor(head_col[:, 3:4], head_col[:, 0:1], head_col[:, 1:2], ALU.mult).then_inc(prep_col, 1)
                dve.wait_ge(prep_col, 1)
                dve.tensor_tensor(head_col[:, 1:2], head_col[:, 3:4], head_col[:, 2:3], ALU.add).then_inc(prep_col, 1)
                dve.wait_ge(prep_col, 2)
                dve.tensor_scalar(s_col[0:R_TOP, 0:1], head_col[:, 1:2], 0.0, None, ALU.max).then_inc(prep_col, 1)
                dve.tensor_scalar(tail_col[:, 2:3], tail_col[:, 1:2], 0.0, None, ALU.max).then_inc(prep_col, 1)
                dve.wait_ge(prep_col, 4)
                dve.tensor_tensor(tail_col[:, 1:2], tail_col[:, 0:1], tail_col[:, 2:3], ALU.mult).then_inc(prep_col, 1)
                dve.tensor_scalar(g8[:], g_col[:], float(C) ** 0.5, None, ALU.mult).then_inc(prep_col, 1)
                dve.tensor_copy(ident_r[:], ident[:]).then_inc(prep_col, 1)
                dve.memset(VO[:], 0.0).then_inc(prep_col, 1)
                dve.wait_ge(prep_col, 8)

            c_high(0)
            dve.wait_ge(const_a, 4)
            prep(prep_runs[0])

            def k_maximum(q, u):
                dve.wait_ge(k_logits, U * q + u + 1)
                dve.tensor_reduce(nm_k[:, u:u + 1], ps_kl[:], AX.X, ALU.max, negate=True).then_inc(k_max, 1)

            def q_maximum(q, u):
                dve.wait_ge(q_logits, U * q + u + 1)
                dve.tensor_reduce(nm_q[u % 2][:], ps_ql[:].rearrange("p (h d) -> p h d", h=HEADS), AX.X, ALU.max,
                                  negate=True).then_inc(q_max, 1)

            def q_total(q, u):
                v = U * q + u
                dve.wait_ge(q_exp, v + 1)
                dve.tensor_reduce(sum_q[u % 4][:], eq[u % 4][:], AX.X, ALU.add).then_inc(q_sum, 1)
                dve.wait_ge(q_sum, v + 1)
                dve.reciprocal(rq[u % 4][:], sum_q[u % 4][:]).then_inc(q_rec, 1)

            def step(p, par):
                q_fin, q_ffn = p - 2, p - 3
                for u in range(U):
                    if on(p):
                        q_maximum(p, u)
                    if on(p + 1):
                        k_maximum(p + 1, u)
                    if u > 0 and on(p):
                        q_total(p, u - 1)
                    if u == 0 and on(p - 1):
                        q_total(p - 1, U - 1)
                    if u == 0 and on(p + 1):
                        x_stats(p + 1)
                    if u == 1 and on(q_fin):
                        dve.wait_ge(ssq_done, q_fin + 1)
                        dve.tensor_scalar(ssq_c[:], ps_x1[:, 0:2 * CHUNKS].rearrange("p (j b) -> p j b", b=2),
                                          NORM_EPS ** 2, None, ALU.max).then_inc(ssq_ok, 1)
                    if u == 1 and on(p + 1):
                        x_normal(p + 1)
                        x_high(p + 1)
                    if u == 2 and on(p + 2):
                        c_high(p + 2)
                    if u == 2 and on(p):
                        dve.wait_ge(m_done, 4 * (p + 1))
                        dve.tensor_copy(M_sb[:], ps_m[:]).then_inc(m_sb, 1)
                        dve.reciprocal(rk[:], sum_k[par][:]).then_inc(rk_ok, 1)
                    if u == 3 and on(q_ffn):
                        dve.wait_ge(ffn_done, q_ffn + 1)
                        dve.wait_ge(x1b_ok, q_ffn + 1)
                        wait(dve, y_out, 16 * q_ffn)
                        dve.tensor_tensor(y[:], ps_x0[:], x1b[:], ALU.add).then_inc(y_ok, 1)
                    if u == 3 and on(q_fin):
                        dve.wait_ge(rn_bc, q_fin + 1)
                        dve.tensor_tensor(on_sb[:], ps_x1[:], o_sb[:], ALU.mult).then_inc(on_ok, 1)
                    if u == 4 and on(q_fin):
                        dve.wait_ge(on_ok, q_fin + 1)
                        dve.wait_ge(xres_in, 16 * (q_fin + 1))
                        wait(dve, x1b_ok, q_fin)
                        dve.scalar_tensor_tensor(out=x1[:], in0=on_sb[:], scalar=g8[:], in1=xres[:], op0=ALU.mult,
                                                 op1=ALU.add).then_inc(x1_ok, 1)
                        dve.wait_ge(x1_ok, q_fin + 1)
                        dve.bn_stats(st2[:], x1[:])
                        dve.drain()
                        dve.bn_aggr(mv2[:], st2[:]).then_inc(z_mv, 1)
                        dve.wait_ge(z_mv, q_fin + 1)
                        dve.tensor_scalar(var2[:], mv2[:, 1:2], LN_EPS, None, ALU.add).then_inc(z_var, 1)
                    if u == 5 and on(p):
                        dve.wait_ge(rk_ok, p + 1)
                        dve.wait_ge(g_done, p + 1)
                        wait(dve, o_done, 4 * (p - 1))
                        dve.tensor_tensor(G_sb[par][:], ps_x0[:].rearrange("p (t b o) -> p t b o", t=TILES, b=2),
                                          rk[:].unsqueeze(3).to_broadcast([P, TILES, 2, C]), ALU.mult).then_inc(g_sb, 1)
                    if u == 5 and on(q_fin):
                        dve.wait_ge(z_rs, q_fin + 1)
                        dve.tensor_scalar(x1hat[:], x1[:], mv2[:, 0:1], rstd2[:], ALU.subtract, ALU.mult)\
                           .then_inc(z_ok, 1)
                    if u == 7 and on(q_fin):
                        dve.wait_ge(z_hi, q_fin + 1)
                        dve.tensor_tensor(zT_lo[:], ps_x1[:].rearrange("p (i s) -> p i s", i=4), zT_hi[:],
                                          ALU.subtract).then_inc(z_lo, 1)
                    if isinstance(p, int) and p == -1:
                        if u == 0:
                            scale_columns()
                        for n in range(2 * u + 1, min(2 * u + 3, N_PREP)):
                            prep(prep_runs[n])

            steps(dve, step)


_INS = ['x', 'ctx_4096', 'L0_xattn_Wq', 'L0_xattn_Wk', 'L0_xattn_Wv', 'L0_xattn_Wo', 'L0_xattn_bo', 'L0_xattn_g',
        'L0_ffn_U_top', 'L0_ffn_S_top', 'L0_ffn_Vh_top', 'L0_ffn_U_tail', 'L0_ffn_S_tail', 'L0_ffn_Vh_tail',
        'L0_ffn_U_tail_r', 'L0_ffn_S_tail_r', 'L0_ffn_Vh_tail_r', 'L0_ffn_alpha', 'L0_ffn_beta', 'L0_ffn_D',
        'L0_ffn_R', 'L0_ffn_bias']
_OUTS = [((32, 64, 512), 'float32')]


def kernel(**inputs):
    import numpy as _np
    import concourse.bacc as _bacc
    from concourse import mybir as _mybir
    from concourse.bass_utils import run_bass_kernel_spmd as _run

    nc = _bacc.Bacc("TRN2", target_bir_lowering=False, num_devices=1)
    arrays, args = {}, []
    for name in _INS:
        a = _np.ascontiguousarray(inputs[name])
        arrays[f"in_{name}_dram"] = a
        args.append(nc.dram_tensor(f"in_{name}_dram", a.shape, _mybir.dt.from_np(a.dtype), kind="ExternalInput").ap())
    for i, (shape, dtype) in enumerate(_OUTS):
        dt = _mybir.dt.from_np(_np.dtype(dtype))
        args.append(nc.dram_tensor(f"out_{i}_dram", shape, dt, kind="ExternalOutput").ap())
    xattn_ffn(nc, *args)
    r = _run(nc, [arrays], core_ids=[0])
    got = tuple(r.results[0][f"out_{i}_dram"] for i in range(len(_OUTS)))
    return got[0]
```

```python
from contextlib import ExitStack

import concourse.bass as bass
from concourse import mybir

ALU = mybir.AluOpType
ACT = mybir.ActivationFunctionType
AX = mybir.AxisListType
F32 = mybir.dt.float32
F32R = mybir.dt.float32r

P = 128
BATCH, C, N = 32, 64, 512
HEADS, DH = 8, 64
HID = HEADS * DH
PAIRS = BATCH // 2
TILES = HID // P
CHUNKS = N // P
U = 2 * TILES
R_TOP, R_INT = 64, 4
R_TAIL = N - R_TOP
SCALE = float(DH) ** -0.5
LN_EPS = 1e-5
NORM_EPS = 1e-12
BANK = 512
R_GROUPS = (0, 32, 64)
R_ROWS = R_GROUPS[-1] + R_INT
N_PREP = 15


def xattn_ffn(nc, x, ctx, Wq, Wk, Wv, Wo, bo, g, U_top, S_top, Vh_top, U_tail, S_tail, Vh_tail,
              U_tail_r, S_tail_r, Vh_tail_r, alpha, beta, D, R, bias, out):
    es = ExitStack()
    with es:
        def sb(name, shape, dt=F32):
            return es.enter_context(nc.sbuf_tensor(name, shape, dt))

        def sem(name):
            return es.enter_context(nc.semaphore(name))

        def bank(name):
            return es.enter_context(nc.psum_tensor(name, [P, BANK], F32))

        ps_kl = bank("ps_kl")
        ps_ql = bank("ps_ql")
        ps_kt = bank("ps_kt")
        ps_qt = bank("ps_qt")
        ps_m = bank("ps_m")
        ps_o = bank("ps_o")
        ps_x0 = bank("ps_x0")
        ps_x1 = bank("ps_x1")
        prep_banks = 2 * [ps_o, ps_ql, ps_qt, ps_x0] + [ps_o, ps_ql, ps_qt] + [ps_o, ps_x0, ps_o, ps_o]

        ident = sb("ident", [P, P])
        ident_r = sb("ident_r", [P, P], F32R)
        batch_of = sb("batch_of", [P, 2])
        minus_half = sb("minus_half", [P, 2 * CHUNKS])
        U_sb = sb("U_sb", [P, 4, N])
        Ur_sb = sb("Ur_sb", [P, 4, R_INT])
        UT_hi = sb("UT_hi", [P, 4, N], F32R)
        UT_lo = sb("UT_lo", [P, 4, N], F32R)
        Vh_sb = sb("Vh_sb", [P, 4, N])
        Vh_hi = sb("Vh_hi", [P, 4, N], F32R)
        Vh_lo = sb("Vh_lo", [P, 4, N], F32R)
        Vhr_sb = sb("Vhr_sb", [R_ROWS, N])
        Vhr_r = sb("Vhr_r", [R_ROWS, N], F32R)
        R_sb = sb("R_sb", [R_INT, R_ROWS])
        s_col = sb("s_col", [P, 4])
        head_col = sb("head_col", [R_TOP, 4])
        tail_col = sb("tail_col", [R_INT, 3])
        BmT = sb("BmT", [R_INT, N])
        RBmT = sb("RBmT", [R_ROWS, N], F32R)
        Wff_hi = sb("Wff_hi", [P, 4, N], F32R)
        Wff_lo = sb("Wff_lo", [P, 4, N], F32R)
        Wq_dup = sb("Wq_dup", [P, TILES, 2 * C])
        Wk_dup = sb("Wk_dup", [P, TILES, 2 * C])
        WqT_hi = sb("WqT_hi", [P, HID], F32R)
        WqT_lo = sb("WqT_lo", [P, HID], F32R)
        WkT_hi = sb("WkT_hi", [P, HID], F32R)
        WkT_lo = sb("WkT_lo", [P, HID], F32R)
        Wv_sb = sb("Wv_sb", [P, TILES, C])
        Wo_sb = sb("Wo_sb", [C, HID])
        WoT = sb("WoT", [P, TILES, C])
        VO = sb("VO", [P, HEADS, 2, C])
        g_col = sb("g_col", [P, 1])
        g8 = sb("g8", [P, 1])
        bo_col = sb("bo_col", [P, 1])
        bias_bc = sb("bias_bc", [P, N])

        xin = sb("xin", [P, N])
        cin = sb("cin", [P, N])
        xres = sb("xres", [P, N])
        xhat = sb("xhat", [P, N])
        x_hi = sb("x_hi", [P, N], F32R)
        x_lo = sb("x_lo", [P, N], F32R)
        c_hi = sb("c_hi", [P, N], F32R)
        c_lo = sb("c_lo", [P, N], F32R)
        xs = [sb(f"xs{i}", [P, 2, N], F32R) for i in range(2)]
        cs = [sb(f"cs{i}", [P, 2, N], F32R) for i in range(2)]
        ctxT = [sb(f"ctxT{i}", [P, CHUNKS, P]) for i in range(2)]
        st1 = sb("st1", [P, 6])
        mv1 = sb("mv1", [P, 2])
        var1 = sb("var1", [P, 1])
        rstd1 = sb("rstd1", [P, 1])
        nm_k = sb("nm_k", [P, U])
        sum_k = [sb(f"sum_k{i}", [P, TILES, 2]) for i in range(2)]
        rk = sb("rk", [P, TILES, 2])
        ek = [sb(f"ek{i}", [P, N]) for i in range(2)]
        ekT = [sb(f"ekT{i}", [P, CHUNKS, P]) for i in range(4)]
        nm_q = [sb(f"nm_q{i}", [P, HEADS], F32R) for i in range(2)]
        eq = [sb(f"eq{i}", [P, HEADS, DH]) for i in range(4)]
        sum_q = [sb(f"sum_q{i}", [P, HEADS]) for i in range(4)]
        rq = [sb(f"rq{i}", [P, HEADS]) for i in range(4)]
        qn = [sb(f"qn{i}", [P, HEADS, DH]) for i in range(4)]
        qT = [sb(f"qT{i}", [P, TILES, P]) for i in range(8)]
        M_sb = sb("M_sb", [P, HID])
        G_sb = [sb(f"G_sb{i}", [P, TILES, 2, C]) for i in range(2)]
        o_sb = sb("o_sb", [P, N])
        o_sq = sb("o_sq", [P, N])
        ssq_c = sb("ssq_c", [P, CHUNKS, 2])
        rnorm = sb("rnorm", [P, CHUNKS, 2])
        on_sb = sb("on_sb", [P, N])
        x1 = sb("x1", [P, N])
        x1b = sb("x1b", [P, N])
        st2 = sb("st2", [P, 6])
        mv2 = sb("mv2", [P, 2])
        var2 = sb("var2", [P, 1])
        rstd2 = sb("rstd2", [P, 1])
        x1hat = sb("x1hat", [P, N])
        zT_hi = sb("zT_hi", [P, 4, P], F32R)
        zT_lo = sb("zT_lo", [P, 4, P], F32R)
        y = sb("y", [P, N])

        wk_in = sem("wk_in")
        wq_in = sem("wq_in")
        wo_in = sem("wo_in")
        wv_in = sem("wv_in")
        u_in = sem("u_in")
        s_in = sem("s_in")
        v_in = sem("v_in")
        r_in = sem("r_in")
        b_in = sem("b_in")
        vh_s, vh_hi, vh_lo = sem("vh_s"), sem("vh_hi"), sem("vh_lo")
        const_a = sem("const_a")
        prep_col = sem("prep_col")
        prep_mm = sem("prep_mm")
        prep_sb = sem("prep_sb")
        prep_hi = sem("prep_hi")
        xin_in, cin_in, xres_in = sem("xin_in"), sem("cin_in"), sem("xres_in")
        x_mv, x_var, x_rs, x_hat = sem("x_mv"), sem("x_var"), sem("x_rs"), sem("x_hat")
        x_hi_ok, x_lo_ok, c_hi_ok, c_lo_ok = sem("x_hi_ok"), sem("x_lo_ok"), sem("c_hi_ok"), sem("c_lo_ok")
        xs_in, cs_in = sem("xs_in"), sem("cs_in")
        k_logits, k_max, k_exp = sem("k_logits"), sem("k_max"), sem("k_exp")
        k_tr, k_trsb = sem("k_tr"), sem("k_trsb")
        ctx_tr, ctx_trsb = sem("ctx_tr"), sem("ctx_trsb")
        m_done, m_sb, rk_ok = sem("m_done"), sem("m_sb"), sem("rk_ok")
        g_done, g_sb = sem("g_done"), sem("g_sb")
        q_logits, q_max, q_shift, q_exp = sem("q_logits"), sem("q_max"), sem("q_shift"), sem("q_exp")
        q_sum, q_rec, q_norm, q_tr, q_trsb = sem("q_sum"), sem("q_rec"), sem("q_norm"), sem("q_tr"), sem("q_trsb")
        o_done, o_ok, sq_ok, ssq_done = sem("o_done"), sem("o_ok"), sem("sq_ok"), sem("ssq_done")
        ssq_ok, rn_ok, rn_bc = sem("ssq_ok"), sem("rn_ok"), sem("rn_bc")
        on_ok, x1_ok, x1b_ok = sem("on_ok"), sem("x1_ok"), sem("x1b_ok")
        z_mv, z_var, z_rs, z_ok = sem("z_mv"), sem("z_var"), sem("z_rs"), sem("z_ok")
        z_tr, z_hi, z_lo = sem("z_tr"), sem("z_hi"), sem("z_lo")
        ffn_done, y_ok, y_out = sem("ffn_done"), sem("y_ok"), sem("y_out")

        x_d = x.rearrange("(q b) c n -> q (b c) n", b=2)
        ctx_d = ctx.rearrange("(q b) c n -> q (b c) n", b=2)
        out_d = out.rearrange("(q b) c n -> q (b c) n", b=2)

        def wait(eng, s, value):
            if isinstance(value, int) and value <= 0:
                return
            eng.wait_ge(s, value)

        def upto(count, last=PAIRS):
            return min(count, last) if isinstance(count, int) else count

        def on(q):
            return not isinstance(q, int) or 0 <= q < PAIRS

        def shifted_by_dve(q, u):
            return u < 3 and (not isinstance(q, int) or 2 <= q < PAIRS - 1)

        def steps(eng, step):
            for p in range(-1, 3):
                step(p, p % 2)
            with eng.Fori(1, PAIRS // 2 - 2) as i:
                step(2 * i + 1, 1)
                step(2 * i + 2, 0)
            for p in range(PAIRS - 3, PAIRS):
                step(p, p % 2)

        Y, Z, L = PAIRS - 3, PAIRS - 2, PAIRS - 1

        first_runs = {(-1, 0): (3, 4), (-1, 1): (5,), (-1, 2): (6, 7), (-1, 3): (8, 9), (-1, 4): (10,)}
        w_eff_runs = {(-1, 5): (0, 0), (-1, 6): (0, 1), (-1, 7): (1, 0), (0, 0): (1, 1),
                      (0, 1): (2, 0), (0, 2): (2, 1), (0, 4): (3, 0), (0, 5): (3, 1)}

        block = es.enter_context(nc.Block())

        U_LOADS, S_LOADS, V_LOADS, R_LOADS, B_LOADS = 2, 9, 3, 7, 5

        @block.sync
        def _(sp):
            def load(dst, src, s):
                sp.dma_start(dst, src).then_inc(s, 16)

            def col(v):
                return v.rearrange("(n a) -> n a", a=1)

            def load_cin(q):
                wait(sp, c_lo_ok, q)
                wait(sp, c_hi_ok, q)
                wait(sp, ctx_tr, q)
                sp.dma_start(cin[:], ctx_d[q]).then_inc(cin_in, 16)

            def load_xin(q):
                wait(sp, x_hat, q)
                sp.dma_start(xin[:], x_d[q]).then_inc(xin_in, 16)

            def stack(q, par, hi, lo, hi_ok, lo_ok, dst, landed):
                wait(sp, hi_ok, q + 1)
                wait(sp, lo_ok, q + 1)
                for b in range(2):
                    sp.dma_start(dst[par][0:C, b, :].bitcast(F32), hi[b * C:(b + 1) * C, :].bitcast(F32)).then_inc(landed, 16)
                    sp.dma_start(dst[par][C:P, b, :].bitcast(F32), lo[b * C:(b + 1) * C, :].bitcast(F32)).then_inc(landed, 16)

            def load_twice(dst, src, s):
                for d in range(2):
                    load(dst[:, :, d * C:(d + 1) * C], src.rearrange("(t p) c -> p t c", p=P), s)

            load(cin[:], ctx_d[0], cin_in)
            load_twice(Wk_dup, Wk, wk_in)
            load(xin[:], x_d[0], xin_in)
            load_twice(Wq_dup, Wq, wq_in)
            load(Wo_sb[:], Wo, wo_in)
            stack(0, 0, c_hi, c_lo, c_hi_ok, c_lo_ok, cs, cs_in)
            load(Wv_sb[:], Wv.rearrange("(t p) c -> p t c", p=P), wv_in)
            load(U_sb[:, :, 0:R_TOP], U_top.rearrange("(t p) r -> p t r", p=P), u_in)
            load(U_sb[:, :, R_TOP:N], U_tail.rearrange("(t p) r -> p t r", p=P), u_in)
            load(head_col[:, 0:1], col(S_top), s_in)
            load(head_col[:, 1:2], col(alpha), s_in)
            load(head_col[:, 2:3], col(beta), s_in)
            load(s_col[R_TOP:P, 0:1], col(S_tail[0:P - R_TOP]), s_in)
            for t in range(1, 4):
                load(s_col[:, t:t + 1], col(S_tail[t * P - R_TOP:(t + 1) * P - R_TOP]), s_in)
            load(tail_col[:, 0:1], col(S_tail_r), s_in)
            load(tail_col[:, 1:2], col(D), s_in)
            load(Vh_sb[0:R_TOP, 0, :], Vh_top, v_in)
            load(Vh_sb[R_TOP:P, 0, :], Vh_tail[0:P - R_TOP, :], v_in)
            load(Vh_sb[:, 1:4, :], Vh_tail[P - R_TOP:R_TAIL, :].rearrange("(t p) i -> p t i", p=P), v_in)
            load(Ur_sb[:], U_tail_r.rearrange("(t p) r -> p t r", p=P), r_in)
            sp.wait_ge(const_a, 8)
            for at in R_GROUPS:
                load(R_sb[:, at:at + R_INT], R, r_in)
                load(Vhr_sb[at:at + R_INT, :], Vh_tail_r, r_in)
            for b in range(2):
                load(bo_col[b * C:(b + 1) * C, :], col(bo), b_in)
                load(g_col[b * C:(b + 1) * C, :], g[0], b_in)
            load(bias_bc[:], bias.rearrange("(a n) -> a n", a=1).to_broadcast([P, N]), b_in)

            def step(p, par):
                if on(p + 2):
                    load_cin(p + 2)
                    load_xin(p + 2)
                if on(p + 1):
                    stack(p + 1, 1 - par, x_hi, x_lo, x_hi_ok, x_lo_ok, xs, xs_in)
                if on(p + 2):
                    stack(p + 2, par, c_hi, c_lo, c_hi_ok, c_lo_ok, cs, cs_in)
                if on(p - 3):
                    store(p - 3)
                if on(p - 1):
                    load_xres(p - 1)

            def store(q):
                sp.wait_ge(y_ok, q + 1)
                sp.dma_start(out_d[q], y[:]).then_inc(y_out, 16)

            def load_xres(q):
                wait(sp, x1_ok, q)
                sp.dma_start(xres[:], x_d[q]).then_inc(xres_in, 16)

            steps(sp, step)
            load_xres(L)
            store(Y)
            store(Z)
            store(L)
            sp.wait_ge(y_out, 16 * PAIRS)

        @block.gpsimd
        def _(pool):
            pool.memset(ident[:], 0.0).then_inc(const_a, 1)
            pool.memset(batch_of[:], 0.0).then_inc(const_a, 1)
            pool.memset(minus_half[:], -0.5).then_inc(const_a, 1)
            pool.wait_ge(const_a, 3)
            pool.affine_select(out=ident[:], in_=ident[:], compare_op=ALU.not_equal, fill=1.0, base=0,
                               pattern=[[-1, P]], channel_multiplier=1).then_inc(const_a, 1)
            for b in range(2):
                pool.wait_ge(const_a, 4 + b)
                pool.memset(batch_of[b * C:(b + 1) * C, b:b + 1], 1.0).then_inc(const_a, 1)
            for tile, done in ((Vhr_sb, 7), (R_sb, 8)):
                pool.wait_ge(const_a, done - 1)
                pool.memset(tile[:], 0.0).then_inc(const_a, 1)
            pool.wait_ge(const_a, 8)

            def c_low(q):
                pool.wait_ge(c_hi_ok, q + 1)
                wait(pool, cs_in, 64 * q)
                pool.tensor_tensor(c_lo[:], cin[:], c_hi[:], ALU.subtract).then_inc(c_lo_ok, 1)

            def x_low(q):
                pool.wait_ge(x_hi_ok, q + 1)
                wait(pool, xs_in, 64 * q)
                pool.tensor_tensor(x_lo[:], xhat[:], x_hi[:], ALU.subtract).then_inc(x_lo_ok, 1)

            c_low(0)

            def x_rstd(q):
                pool.wait_ge(x_var, q + 1)
                pool.tensor_tensor(rstd1[:], var1[:], minus_half[:, 0:1], ALU.pow).then_inc(x_rs, 1)

            def norm(q, u):
                v = U * q + u
                pool.wait_ge(q_rec, v + 1)
                wait(pool, q_tr, v - 3)
                pool.tensor_tensor(qn[u % 4][:], eq[u % 4][:], rq[u % 4][:].unsqueeze(2).to_broadcast([P, HEADS, DH]),
                                   ALU.mult).then_inc(q_norm, 1)

            def norm_pow(q):
                pool.wait_ge(ssq_ok, q + 1)
                pool.tensor_tensor(rnorm[:], ssq_c[:], minus_half[:].rearrange("p (j b) -> p j b", b=2),
                                   ALU.pow).then_inc(rn_ok, 1)

            def z_rstd(q):
                pool.wait_ge(z_var, q + 1)
                pool.tensor_tensor(rstd2[:], var2[:], minus_half[:, 0:1], ALU.pow).then_inc(z_rs, 1)

            def x1_bias(q):
                pool.wait_ge(x1_ok, q + 1)
                wait(pool, y_ok, q)
                pool.tensor_tensor(x1b[:], x1[:], bias_bc[:], ALU.add).then_inc(x1b_ok, 1)

            def o_square(q):
                pool.wait_ge(o_ok, q + 1)
                wait(pool, ssq_done, q)
                pool.tensor_tensor(o_sq[:], o_sb[:], o_sb[:], ALU.mult).then_inc(sq_ok, 1)

            def step(p, par):
                for u in range(U):
                    if u > 0 and on(p):
                        norm(p, u - 1)
                    if u == 0 and on(p - 1):
                        norm(p - 1, U - 1)
                    if u == 0 and on(p + 1):
                        x_rstd(p + 1)
                    if u == 1 and on(p - 2):
                        norm_pow(p - 2)
                    if u == 2 and on(p + 1):
                        x_low(p + 1)
                    if u == 3 and on(p + 2) and on(p):
                        c_low(p + 2)
                    if u == 4 and on(p - 2):
                        z_rstd(p - 2)
                    if u == 6 and on(p - 2):
                        x1_bias(p - 2)
                    if u == 7 and on(p - 1):
                        o_square(p - 1)
                    if isinstance(p, int) and p == -1 and u == 5:
                        c_low(1)
                    if isinstance(p, int) and p == -1 and 2 <= u < 6:
                        k = u - 2
                        pool.wait_ge(vh_hi, k + 1)
                        pool.tensor_tensor(Vh_lo[:, k, :], Vh_sb[:, k, :], Vh_hi[:, k, :],
                                           ALU.subtract).then_inc(vh_lo, 1)
                if isinstance(p, int) and p == 0:
                    pool.wait_ge(b_in, 16 * B_LOADS)

            steps(pool, step)
            norm(L, U - 1)
            norm_pow(Z)
            norm_pow(L)
            z_rstd(Z)
            x1_bias(Z)
            z_rstd(L)
            x1_bias(L)

        @block.tensor
        def _(pe):
            def prep(n):
                run, landed, loads, needs = prep_runs[n]
                pe.wait_ge(landed, 16 * loads)
                before = [m + 1 for m in range(n) if prep_banks[m] is prep_banks[n]]
                wait(pe, prep_sb, max([needs] + before))
                run(prep_banks[n]).then_inc(prep_mm, 1)

            def transposes(tiles):
                def run(ps):
                    at = 0
                    for src, rows, cols in tiles:
                        last = pe.transpose(ps[0:cols, at:at + rows], src, ident[0:rows, 0:rows])
                        at += rows
                    return last
                return run

            def wo_wv(half):
                def run(ps):
                    r = slice(half * DH, (half + 1) * DH)
                    for b in range(2):
                        for t in range(TILES):
                            last = pe.matmul(ps[b * C:(b + 1) * C, t * C:(t + 1) * C], Wv_sb[r, t, :], WoT[r, t, :],
                                             start=True, stop=True)
                    return last
                return run

            def w_eff(i, half):
                n = N_PREP - 4 + i
                ps = prep_banks[n]
                if half == 0:
                    wait(pe, prep_sb, max(m + 1 for m in range(n) if prep_banks[m] is ps))
                for k in (2 * half, 2 * half + 1):
                    pe.wait_ge(vh_lo, k + 1)
                    pe.wait_ge(prep_sb, (6, 7, 8, 10)[k])
                    for v, w in ((Vh_hi, UT_hi), (Vh_lo, UT_hi), (Vh_hi, UT_lo)):
                        pe.matmul(ps[:], v[:, k, i * P:(i + 1) * P], w[:, k, :], start=(k == 0 and v is Vh_hi and w is UT_hi),
                                  stop=False)
                if half:
                    pe.wait_ge(prep_sb, 11)
                    pe.matmul(ps[:], Vhr_r[:, i * P:(i + 1) * P], RBmT[:], start=False, stop=True).then_inc(prep_mm, 1)

            prep_runs = [
                (transposes([(Wk_dup[:, t, :], P, P) for t in range(TILES)]), wk_in, 2, 0),
                (transposes([(Wq_dup[:, t, :], P, P) for t in range(TILES)]), wq_in, 2, 0),
                (transposes([(Wo_sb[:, t * P:(t + 1) * P], C, P) for t in range(TILES)]), wo_in, 1, 0),
                (wo_wv(0), wv_in, 1, 3),
                (wo_wv(1), wv_in, 1, 3),
                *[(transposes([(U_sb[:, t, k * P:(k + 1) * P], P, P) for t in range(4)]), u_in, U_LOADS, 0)
                  for k in range(3)],
                (transposes([(Ur_sb[:, t, :], P, R_INT) for t in range(4)]), r_in, R_LOADS, 0),
                (transposes([(U_sb[:, t, 3 * P:4 * P], P, P) for t in range(4)]), u_in, U_LOADS, 0),
                (lambda ps: pe.matmul(ps[0:R_ROWS, :], R_sb[:], BmT[:], start=True, stop=True), r_in, R_LOADS, 9),
            ]
            assert len(prep_runs) == N_PREP - 4
            pe.wait_ge(const_a, 6)
            for n in range(3):
                prep(n)
            pe.wait_ge(prep_sb, 1)

            def k_front(q, u, par):
                t, b = u // 2, u % 2
                v = U * q + u
                if u == 0:
                    pe.wait_ge(cs_in, 64 * (q + 1))
                wait(pe, k_exp, v)
                for w in (WkT_hi, WkT_lo):
                    last = pe.matmul(ps_kl[:], w[:, t * P:(t + 1) * P], cs[par][:, b, :],
                                     start=(w is WkT_hi), stop=(w is WkT_lo))
                last.then_inc(k_logits, 1)

            def k_back(q, u):
                v = U * q + u
                pe.wait_ge(k_exp, v + 1)
                wait(pe, k_trsb, v)
                for j in range(CHUNKS):
                    last = pe.transpose(ps_kt[:, j * P:(j + 1) * P], ek[u % 2][:, j * P:(j + 1) * P], ident[:])
                last.then_inc(k_tr, 1)

            def k_product(q, t, half, par):
                if half == 0:
                    pe.wait_ge(k_trsb, U * q + 2 * t + 2)
                    if t == 0:
                        pe.wait_ge(ctx_trsb, q + 1)
                        wait(pe, m_sb, q)
                for j in (2 * half, 2 * half + 1):
                    for b in range(2):
                        last = pe.matmul(ps_m[b * C:(b + 1) * C, t * P:(t + 1) * P],
                                         ctxT[par][:, j, b * C:(b + 1) * C], ekT[(2 * t + b) % 4][:, j, :],
                                         start=(j == 0), stop=(j == CHUNKS - 1))
                if half:
                    last.then_inc(m_done, 1)

            def ctx_transpose(q):
                pe.wait_ge(cin_in, 16 * (q + 1))
                wait(pe, z_lo, q - 3)
                wait(pe, ctx_trsb, q)
                for j in range(CHUNKS):
                    last = pe.transpose(ps_x1[:, j * P:(j + 1) * P], cin[:, j * P:(j + 1) * P], ident[:])
                last.then_inc(ctx_tr, 1)

            def g_product(q):
                pe.wait_ge(m_sb, q + 1)
                wait(pe, g_sb, q)
                wait(pe, y_ok, q - 2)
                for t in range(TILES):
                    for s in range(2):
                        at = t * P + s * DH
                        last = pe.matmul(ps_x0[s * DH:(s + 1) * DH, t * P:(t + 1) * P], M_sb[:, at:at + DH],
                                         VO[:, 2 * t + s, :, :], start=True, stop=True)
                last.then_inc(g_done, 1)

            def q_front(q, u, par):
                j, b = u // 2, u % 2
                v = U * q + u
                if u == 0:
                    pe.wait_ge(xs_in, 64 * (q + 1))
                wait(pe, q_exp, v)
                for w in (WqT_hi, WqT_lo):
                    last = pe.matmul(ps_ql[:], xs[par][:, b, j * P:(j + 1) * P], w[:],
                                     start=(w is WqT_hi), stop=(w is WqT_lo))
                last.then_inc(q_logits, 1)

            def q_sub(q, u):
                pe.wait_ge(q_max, U * q + u + 1)
                pe.matmul(ps_ql[:], ident_r[:], nm_q[u % 2][:].unsqueeze(2).to_broadcast([P, HEADS, DH]),
                          start=False, stop=True, skip_group_check=True).then_inc(q_shift, 1)

            def q_back(q, u):
                v = U * q + u
                pe.wait_ge(q_norm, v + 1)
                wait(pe, q_trsb, v)
                for t in range(TILES):
                    last = pe.transpose(ps_qt[:, t * P:(t + 1) * P], qn[u % 4][:, 2 * t:2 * t + 2, :], ident[:])
                last.then_inc(q_tr, 1)

            def o_product(q, j, half, par):
                if half == 0:
                    pe.wait_ge(q_trsb, U * q + 2 * j + 2)
                    if j == 0:
                        pe.wait_ge(g_sb, q + 1)
                        wait(pe, o_ok, q)
                for t in (2 * half, 2 * half + 1):
                    for b in range(2):
                        last = pe.matmul(ps_o[b * C:(b + 1) * C, j * P:(j + 1) * P], G_sb[par][:, t, b, :],
                                         qT[2 * j + b][:, t, :], start=(t == 0), stop=(t == TILES - 1))
                if half:
                    last.then_inc(o_done, 1)

            def ssq(q, ps=ps_x1):
                pe.wait_ge(sq_ok, q + 1)
                if ps is ps_x1:
                    pe.wait_ge(ctx_trsb, upto(q + 4))
                    wait(pe, z_lo, q)
                for j in range(CHUNKS):
                    last = pe.matmul(ps[:, 2 * j:2 * j + 2], o_sq[:, j * P:(j + 1) * P], batch_of[:],
                                     start=True, stop=True)
                last.then_inc(ssq_done, 1)

            def norm_rows(q, ps=ps_x1):
                pe.wait_ge(rn_ok, q + 1)
                for j in range(CHUNKS):
                    for b in range(2):
                        last = pe.matmul(ps[b * C:(b + 1) * C, j * P:(j + 1) * P],
                                         rnorm[:, j, b:b + 1].to_broadcast([P, C]), ident[:], start=True, stop=True)
                last.then_inc(rn_bc, 1)

            def z_transpose(q, ps=ps_x1):
                pe.wait_ge(z_ok, q + 1)
                for i in range(4):
                    last = pe.transpose(ps[:, i * P:(i + 1) * P], x1hat[:, i * P:(i + 1) * P], ident[:])
                last.then_inc(z_tr, 1)

            def ffn(q, half, ps=ps_x0):
                if half == 0:
                    pe.wait_ge(z_lo, q + 1)
                    if ps is ps_x0:
                        pe.wait_ge(g_sb, upto(q + 3))
                        wait(pe, y_ok, q)
                for i in (2 * half, 2 * half + 1):
                    for z, w in ((zT_hi, Wff_hi), (zT_lo, Wff_hi), (zT_hi, Wff_lo)):
                        last = pe.matmul(ps[:], z[:, i, :], w[:, i, :], start=(i == 0 and z is zT_hi and w is Wff_hi),
                                         stop=(i == 3 and w is Wff_lo))
                if half:
                    last.then_inc(ffn_done, 1)

            def step(p, par):
                for u in range(U):
                    if u == 1 and on(p - 2):
                        ssq(p - 2)
                    if on(p):
                        q_front(p, u, par)
                    if on(p + 1):
                        k_front(p + 1, u, 1 - par)
                    if u > 0 and on(p + 1):
                        k_back(p + 1, u - 1)
                    if u == 0 and on(p):
                        k_back(p, U - 1)
                    if u == 0 and on(p + 1):
                        ctx_transpose(p + 1)
                    if u == 6 and on(p - 2):
                        z_transpose(p - 2)
                    if u > 1 and on(p):
                        q_back(p, u - 2)
                    if u < 2 and on(p - 1):
                        q_back(p - 1, U - 2 + u)
                    if on(p) and on(p + 1) and not shifted_by_dve(p, u):
                        q_sub(p, u)
                    if u in (1, 2) and on(p - 3):
                        ffn(p - 3, u - 1)
                    if u >= 3 and on(p + 1):
                        k_product(p + 1, (u - 3) // 2, (u - 3) % 2, 1 - par)
                    if u < 3 and on(p):
                        k_product(p, (u + 5) // 2, (u + 5) % 2, par)
                    if u == 7 and on(p):
                        if isinstance(p, int) and p == 0:
                            pe.wait_ge(prep_sb, N_PREP)
                        o_product(p, 0, 0, par)
                    if u < 7 and on(p - 1):
                        o_product(p - 1, (u + 1) // 2, (u + 1) % 2, 1 - par)
                    if on(p) and not on(p + 1):
                        q_sub(p, u)
                    if u == 4 and on(p):
                        if isinstance(p, int) and p == 0:
                            pe.wait_ge(prep_sb, 13)
                        g_product(p)
                    if u == 2 and on(p - 2):
                        norm_rows(p - 2)
                    if isinstance(p, int):
                        for n in first_runs.get((p, u), ()):
                            prep(n)
                        if (p, u) in w_eff_runs:
                            w_eff(*w_eff_runs[p, u])
                if isinstance(p, int) and p == -1:
                    pe.wait_ge(prep_sb, N_PREP - 4)

            steps(pe, step)
            ffn(Y, 0)
            q_back(L, U - 2)
            o_product(L, 0, 1, L % 2)
            o_product(L, 1, 0, L % 2)
            o_product(L, 1, 1, L % 2)
            ssq(Z)
            q_back(L, U - 1)
            o_product(L, 2, 0, L % 2)
            o_product(L, 2, 1, L % 2)
            o_product(L, 3, 0, L % 2)
            o_product(L, 3, 1, L % 2)
            norm_rows(Z)
            ssq(L, ps_kl)
            ffn(Y, 1)
            norm_rows(L, ps_kl)
            z_transpose(Z)
            ffn(Z, 0)
            ffn(Z, 1)
            z_transpose(L, ps_kt)
            ffn(L, 0, ps_m)
            ffn(L, 1, ps_m)

        @block.scalar
        def _(act):
            def k_exponent(q, u, par):
                t, b = u // 2, u % 2
                v = U * q + u
                act.wait_ge(k_max, v + 1)
                wait(act, k_tr, v - 1)
                if u == 0:
                    wait(act, rk_ok, q - 1)
                act.activation(ek[u % 2][:], ps_kl[:], ACT.Exp, bias=nm_k[:, u:u + 1],
                               accum_out=sum_k[par][:, t, b:b + 1]).then_inc(k_exp, 1)

            def k_copy(q, u):
                v = U * q + u
                act.wait_ge(k_tr, v + 1)
                wait(act, m_done, 4 * q + u // 2 - 1)
                act.activation(ekT[u % 4][:], ps_kt[:], ACT.Copy).then_inc(k_trsb, 1)

            def q_exponent(q, u):
                v = U * q + u
                act.wait_ge(q_shift, v + 1)
                wait(act, q_norm, v - 3)
                act.activation(eq[u % 4][:], eq[u % 4][:] if shifted_by_dve(q, u) else ps_ql[:], ACT.Exp).then_inc(q_exp, 1)

            def q_copy(q, u):
                v = U * q + u
                act.wait_ge(q_tr, v + 1)
                wait(act, o_done, 4 * (q - 1) + u // 2 + 1)
                act.activation(qT[u][:], ps_qt[:], ACT.Copy).then_inc(q_trsb, 1)

            def o_bias(q):
                act.wait_ge(o_done, 4 * (q + 1))
                wait(act, on_ok, q)
                wait(act, sq_ok, q)
                act.activation(o_sb[:], ps_o[:], ACT.Identity, bias=bo_col[:]).then_inc(o_ok, 1)

            def z_high(q, ps=ps_x1):
                act.wait_ge(z_tr, q + 1)
                wait(act, ffn_done, q)
                act.activation(zT_hi[:], ps[:], ACT.Copy).then_inc(z_hi, 1)

            def step(p, par):
                for u in range(U):
                    if u == 7 and on(p - 1):
                        o_bias(p - 1)
                    if u > 0 and on(p + 1):
                        k_copy(p + 1, u - 1)
                    if u == 0 and on(p):
                        k_copy(p, U - 1)
                    if u == 0 and on(p + 1):
                        act.wait_ge(ctx_tr, p + 2)
                        wait(act, m_done, 4 * p)
                        act.activation(ctxT[1 - par][:], ps_x1[:], ACT.Copy).then_inc(ctx_trsb, 1)
                    if on(p):
                        q_exponent(p, u)
                    if on(p + 1):
                        k_exponent(p + 1, u, 1 - par)
                    if u > 1 and on(p):
                        q_copy(p, u - 2)
                    if u < 2 and on(p - 1):
                        q_copy(p - 1, U - 2 + u)
                    if u == 2 and on(p):
                        act.wait_ge(m_done, 4 * (p + 1))
                        wait(act, g_done, p)
                        act.activation(M_sb[:], ps_m[:], ACT.Copy).then_inc(m_sb, 1)
                    if u == 6 and on(p - 2):
                        z_high(p - 2)
                    if isinstance(p, int) and p == -1 and 2 <= u < 6:
                        k = u - 2
                        act.wait_ge(v_in, 16 * V_LOADS)
                        act.wait_ge(prep_col, 7)
                        act.activation(Vh_sb[:, k, :], Vh_sb[:, k, :], ACT.Copy, scale=s_col[:, k:k + 1]).then_inc(vh_s, 1)
                        act.wait_ge(vh_s, k + 1)
                        act.activation(Vh_hi[:, k, :], Vh_sb[:, k, :], ACT.Copy).then_inc(vh_hi, 1)
                if isinstance(p, int) and p == 0:
                    act.wait_ge(b_in, 16 * B_LOADS)

            steps(act, step)
            q_copy(L, U - 2)
            q_copy(L, U - 1)
            act.wait_ge(o_done, 4 * (L + 1))
            act.wait_ge(x_lo_ok, L + 1)
            act.activation(xhat[:], ps_o[:], ACT.Identity, bias=bo_col[:]).then_inc(o_ok, 1)
            act.wait_ge(o_ok, L + 1)
            act.wait_ge(ssq_done, L)
            act.activation(o_sq[:], xhat[:], ACT.Square).then_inc(sq_ok, 1)
            z_high(Z)
            z_high(L, ps_kt)

        @block.vector
        def _(dve):
            def c_high(q):
                dve.wait_ge(cin_in, 16 * (q + 1))
                wait(dve, cs_in, 64 * q)
                dve.tensor_copy(c_hi[:], cin[:]).then_inc(c_hi_ok, 1)

            def x_stats(q):
                dve.wait_ge(xin_in, 16 * (q + 1))
                dve.bn_stats(st1[:], xin[:])
                dve.drain()
                dve.bn_aggr(mv1[:], st1[:]).then_inc(x_mv, 1)
                dve.wait_ge(x_mv, q + 1)
                dve.tensor_scalar(var1[:], mv1[:, 1:2], LN_EPS, None, ALU.add).then_inc(x_var, 1)

            def x_normal(q):
                dve.wait_ge(x_rs, q + 1)
                wait(dve, x_lo_ok, q)
                dve.tensor_scalar(xhat[:], xin[:], mv1[:, 0:1], rstd1[:], ALU.subtract, ALU.mult).then_inc(x_hat, 1)

            def x_high(q):
                dve.wait_ge(x_hat, q + 1)
                wait(dve, xs_in, 64 * q)
                dve.tensor_copy(x_hi[:], xhat[:]).then_inc(x_hi_ok, 1)

            n_hi = [0]

            def split(ps, hi, lo):
                dve.tensor_copy(hi, ps).then_inc(prep_hi, 1)
                n_hi[0] += 1
                dve.wait_ge(prep_hi, n_hi[0])
                return dve.tensor_tensor(lo, ps, hi, ALU.subtract)

            def prep(n):
                dve.wait_ge(prep_mm, n + 1)
                prep_runs[n](prep_banks[n]).then_inc(prep_sb, 1)

            def vo_block(ps, half):
                for b in range(2):
                    r = slice(b * C, (b + 1) * C)
                    last = dve.tensor_scalar(VO[:].rearrange("p (t s) a o -> p t s a o", s=2)[r, :, half, b, :],
                                             ps[r, 0:TILES * C].rearrange("p (t o) -> p t o", t=TILES),
                                             SCALE, None, ALU.mult)
                return last

            def rank_groups(ps):
                at = R_GROUPS[1]
                dve.wait_ge(r_in, 16 * R_LOADS)
                dve.tensor_copy(Vhr_r[:], Vhr_sb[:]).then_inc(prep_hi, 1)
                dve.tensor_copy(RBmT[:], ps[0:R_ROWS, :]).then_inc(prep_hi, 1)
                n_hi[0] += 2
                dve.wait_ge(prep_hi, n_hi[0])
                dve.tensor_tensor(Vhr_r[at:at + R_INT, :], Vhr_sb[at:at + R_INT, :], Vhr_r[at:at + R_INT, :],
                                  ALU.subtract)
                at = R_GROUPS[2]
                return dve.tensor_tensor(RBmT[at:at + R_INT, :], ps[at:at + R_INT, :], RBmT[at:at + R_INT, :],
                                         ALU.subtract)

            prep_runs = [
                lambda ps: split(ps[:], WkT_hi[:], WkT_lo[:]),
                lambda ps: split(ps[:], WqT_hi[:], WqT_lo[:]),
                lambda ps: dve.tensor_copy(WoT[:], ps[:, 0:TILES * C].rearrange("p (t o) -> p t o", t=TILES)),
                lambda ps: vo_block(ps, 0),
                lambda ps: vo_block(ps, 1),
                *[lambda ps, k=k: split(ps[:], UT_hi[:, k, :], UT_lo[:, k, :]) for k in range(3)],
                lambda ps: dve.tensor_scalar(BmT[:], ps[0:R_INT, :], tail_col[:, 1:2], None, ALU.mult),
                lambda ps: split(ps[:], UT_hi[:, 3, :], UT_lo[:, 3, :]),
                lambda ps: rank_groups(ps),
                *[lambda ps, i=i: split(ps[:], Wff_hi[:, i, :], Wff_lo[:, i, :]) for i in range(4)],
            ]

            def scale_columns():
                dve.wait_ge(s_in, 16 * S_LOADS)
                dve.tensor_tensor(head_col[:, 3:4], head_col[:, 0:1], head_col[:, 1:2], ALU.mult).then_inc(prep_col, 1)
                dve.wait_ge(prep_col, 3)
                dve.tensor_tensor(head_col[:, 1:2], head_col[:, 3:4], head_col[:, 2:3], ALU.add).then_inc(prep_col, 1)
                dve.wait_ge(prep_col, 4)
                dve.tensor_scalar(s_col[0:R_TOP, 0:1], head_col[:, 1:2], 0.0, None, ALU.max).then_inc(prep_col, 1)
                dve.tensor_scalar(tail_col[:, 2:3], tail_col[:, 1:2], 0.0, None, ALU.max).then_inc(prep_col, 1)
                dve.wait_ge(prep_col, 6)
                dve.tensor_tensor(tail_col[:, 1:2], tail_col[:, 0:1], tail_col[:, 2:3], ALU.mult).then_inc(prep_col, 1)
                dve.wait_ge(prep_col, 7)

            dve.memset(VO[:], 0.0).then_inc(prep_col, 1)
            c_high(0)
            dve.wait_ge(const_a, 4)
            dve.tensor_copy(ident_r[:], ident[:]).then_inc(prep_col, 1)
            dve.wait_ge(prep_col, 2)
            for n in range(3):
                prep(n)

            def k_maximum(q, u):
                dve.wait_ge(k_logits, U * q + u + 1)
                dve.tensor_reduce(nm_k[:, u:u + 1], ps_kl[:], AX.X, ALU.max, negate=True).then_inc(k_max, 1)

            def q_maximum(q, u):
                dve.wait_ge(q_logits, U * q + u + 1)
                dve.tensor_reduce(nm_q[u % 2][:], ps_ql[:].rearrange("p (h d) -> p h d", h=HEADS), AX.X, ALU.max,
                                  negate=True).then_inc(q_max, 1)
                if shifted_by_dve(q, u):
                    dve.wait_ge(q_max, U * q + u + 1)
                    wait(dve, q_norm, U * q + u - 3)
                    dve.tensor_tensor(eq[u % 4][:], ps_ql[:].rearrange("p (h d) -> p h d", h=HEADS),
                                      nm_q[u % 2][:].bitcast(F32).unsqueeze(2).to_broadcast([P, HEADS, DH]),
                                      ALU.add).then_inc(q_shift, 1)

            def q_total(q, u):
                v = U * q + u
                dve.wait_ge(q_exp, v + 1)
                dve.tensor_reduce(sum_q[u % 4][:], eq[u % 4][:], AX.X, ALU.add).then_inc(q_sum, 1)
                dve.wait_ge(q_sum, v + 1)
                dve.reciprocal(rq[u % 4][:], sum_q[u % 4][:]).then_inc(q_rec, 1)

            def ssq_clamp(q, ps=ps_x1):
                dve.wait_ge(ssq_done, q + 1)
                dve.tensor_scalar(ssq_c[:], ps[:, 0:2 * CHUNKS].rearrange("p (j b) -> p j b", b=2),
                                  NORM_EPS ** 2, None, ALU.max).then_inc(ssq_ok, 1)

            def o_normal(q, ps=ps_x1, o=o_sb):
                dve.wait_ge(rn_bc, q + 1)
                dve.tensor_tensor(on_sb[:], ps[:], o[:], ALU.mult).then_inc(on_ok, 1)

            def residual(q):
                dve.wait_ge(on_ok, q + 1)
                dve.wait_ge(xres_in, 16 * (q + 1))
                wait(dve, x1b_ok, q)
                dve.scalar_tensor_tensor(out=x1[:], in0=on_sb[:], scalar=g8[:], in1=xres[:], op0=ALU.mult,
                                         op1=ALU.add).then_inc(x1_ok, 1)
                dve.wait_ge(x1_ok, q + 1)
                dve.bn_stats(st2[:], x1[:])
                dve.drain()
                dve.bn_aggr(mv2[:], st2[:]).then_inc(z_mv, 1)
                dve.wait_ge(z_mv, q + 1)
                dve.tensor_scalar(var2[:], mv2[:, 1:2], LN_EPS, None, ALU.add).then_inc(z_var, 1)

            def z_normal(q):
                dve.wait_ge(z_rs, q + 1)
                dve.tensor_scalar(x1hat[:], x1[:], mv2[:, 0:1], rstd2[:], ALU.subtract, ALU.mult).then_inc(z_ok, 1)

            def z_low(q, ps=ps_x1):
                dve.wait_ge(z_hi, q + 1)
                dve.tensor_tensor(zT_lo[:], ps[:].rearrange("p (i s) -> p i s", i=4), zT_hi[:],
                                  ALU.subtract).then_inc(z_lo, 1)

            def y_sum(q, ps=ps_x0):
                dve.wait_ge(ffn_done, q + 1)
                dve.wait_ge(x1b_ok, q + 1)
                wait(dve, y_out, 16 * q)
                dve.tensor_tensor(y[:], ps[:], x1b[:], ALU.add).then_inc(y_ok, 1)

            def step(p, par):
                for u in range(U):
                    if on(p):
                        q_maximum(p, u)
                    if on(p + 1):
                        k_maximum(p + 1, u)
                    if isinstance(p, int):
                        slot = (p, u - 1) if u else (p - 1, U - 1)
                        for n in first_runs.get(slot, ()):
                            prep(n)
                        if slot == (-1, 1):
                            scale_columns()
                        if w_eff_runs.get(slot, (0, 0))[1]:
                            prep(N_PREP - 4 + w_eff_runs[slot][0])
                    if u > 0 and on(p):
                        q_total(p, u - 1)
                    if u == 0 and on(p - 1):
                        q_total(p - 1, U - 1)
                    if u == 0 and on(p + 1):
                        x_stats(p + 1)
                    if u == 1 and on(p - 2):
                        ssq_clamp(p - 2)
                    if u == 1 and on(p + 1):
                        x_normal(p + 1)
                        x_high(p + 1)
                    if u == 2 and on(p + 2) and on(p):
                        c_high(p + 2)
                    if u == 2 and on(p):
                        dve.wait_ge(k_exp, U * (p + 1))
                        dve.reciprocal(rk[:], sum_k[par][:]).then_inc(rk_ok, 1)
                    if u == 3 and on(p - 3):
                        y_sum(p - 3)
                    if u == 3 and on(p - 2):
                        o_normal(p - 2)
                    if u == 4 and on(p - 2):
                        residual(p - 2)
                    if u == 5 and on(p):
                        dve.wait_ge(rk_ok, p + 1)
                        dve.wait_ge(g_done, p + 1)
                        wait(dve, o_done, 4 * (p - 1))
                        dve.tensor_tensor(G_sb[par][:], ps_x0[:].rearrange("p (t b o) -> p t b o", t=TILES, b=2),
                                          rk[:].unsqueeze(3).to_broadcast([P, TILES, 2, C]), ALU.mult).then_inc(g_sb, 1)
                    if u == 5 and on(p - 2):
                        z_normal(p - 2)
                    if u == 7 and on(p - 2):
                        z_low(p - 2)
                    if isinstance(p, int) and p == -1 and u == 4:
                        c_high(1)
                if isinstance(p, int) and p == 0:
                    dve.wait_ge(b_in, 16 * B_LOADS)
                    dve.tensor_scalar(g8[:], g_col[:], float(C) ** 0.5, None, ALU.mult).then_inc(prep_col, 1)
                    dve.wait_ge(prep_col, 8)

            steps(dve, step)
            q_total(L, U - 1)
            ssq_clamp(Z)
            o_normal(Z)
            ssq_clamp(L, ps_kl)
            residual(Z)
            y_sum(Y)
            z_normal(Z)
            o_normal(L, ps_kl, xhat)
            z_low(Z)
            residual(L)
            z_normal(L)
            y_sum(Z)
            z_low(L, ps_kt)
            y_sum(L, ps_m)


_INS = ['x', 'ctx_4096', 'L0_xattn_Wq', 'L0_xattn_Wk', 'L0_xattn_Wv', 'L0_xattn_Wo', 'L0_xattn_bo', 'L0_xattn_g',
        'L0_ffn_U_top', 'L0_ffn_S_top', 'L0_ffn_Vh_top', 'L0_ffn_U_tail', 'L0_ffn_S_tail', 'L0_ffn_Vh_tail',
        'L0_ffn_U_tail_r', 'L0_ffn_S_tail_r', 'L0_ffn_Vh_tail_r', 'L0_ffn_alpha', 'L0_ffn_beta', 'L0_ffn_D',
        'L0_ffn_R', 'L0_ffn_bias']
_OUTS = [((32, 64, 512), 'float32')]


def kernel(**inputs):
    import numpy as _np
    import concourse.bacc as _bacc
    from concourse import mybir as _mybir
    from concourse.bass_utils import run_bass_kernel_spmd as _run

    nc = _bacc.Bacc("TRN2", target_bir_lowering=False, num_devices=1)
    arrays, args = {}, []
    for name in _INS:
        a = _np.ascontiguousarray(inputs[name])
        arrays[f"in_{name}_dram"] = a
        args.append(nc.dram_tensor(f"in_{name}_dram", a.shape, _mybir.dt.from_np(a.dtype), kind="ExternalInput").ap())
    for i, (shape, dtype) in enumerate(_OUTS):
        dt = _mybir.dt.from_np(_np.dtype(dtype))
        args.append(nc.dram_tensor(f"out_{i}_dram", shape, dt, kind="ExternalOutput").ap())
    xattn_ffn(nc, *args)
    r = _run(nc, [arrays], core_ids=[0])
    got = tuple(r.results[0][f"out_{i}_dram"] for i in range(len(_OUTS)))
    return got[0]
```
